# Optimizing a Trainium2 kernel written in Bass

```python
import numpy as np
import jax
import jax.numpy as jnp

def _softmax(x, axis=-1):
    return jax.nn.softmax(x, axis=axis)

def _gelu(x):
    return jax.nn.gelu(x, approximate=True)

def _silu(x):
    return jax.nn.silu(x)

def _sigmoid(x):
    return jax.nn.sigmoid(x)

def _layernorm(x, axis=-1, eps=1e-05):
    m = jnp.mean(x, axis=axis, keepdims=True)
    v = jnp.var(x, axis=axis, keepdims=True)
    return (x - m) / jnp.sqrt(v + eps)

def _scatter_add(tgt, idx, src, axis=0):
    return tgt.at[idx].add(src)

def _segment_sum(src, seg, n):
    return jax.ops.segment_sum(src, seg, n)
kernel_name = 'mk_recurrent_d1_jaxref_r8_9f6400'

def setup_inputs(seed: int=0):
    np.random.seed(seed)
    _w = jnp.asarray

    def _L0_attn_setup():
        import jax, jax.numpy as jnp
        import numpy as np
        E = 256
        H = 16
        HD = E // H
        CKV = 64
        CQ = 192
        RD = 64
        SCALE = 1.0 / np.sqrt(HD + RD)

        def _rope(qr, kr, offset=0):
            s = qr.shape[2]
            t = jnp.arange(offset, offset + s, dtype=jnp.float32)
            inv_freq = 1.0 / 10000.0 ** (jnp.arange(0, RD, 2, dtype=jnp.float32) / RD)
            freqs = t[:, None] * inv_freq[None, :]
            cos = jnp.concatenate([jnp.cos(freqs)] * 2, axis=-1)
            sin = jnp.concatenate([jnp.sin(freqs)] * 2, axis=-1)

            def rot(x):
                x1, x2 = (x[..., :RD // 2], x[..., RD // 2:])
                return jnp.concatenate([-x2, x1], axis=-1)
            return (qr * cos + rot(qr) * sin, kr * cos + rot(kr) * sin)
        key = jax.random.key(seed)
        ks = jax.random.split(key, 10)

        def w(k, out_d, in_d):
            return jax.random.normal(k, (out_d, in_d), jnp.float32) * (1.0 / np.sqrt(in_d))
        return {'x': jax.random.normal(ks[0], (2, 256, E), jnp.float32), 'w_dq': w(ks[1], CQ, E), 'w_uq': w(ks[2], H * HD, CQ), 'w_dkv': w(ks[3], CKV, E), 'w_uk': w(ks[4], H * HD, CKV), 'w_uv': w(ks[5], H * HD, CKV), 'w_qr': w(ks[6], H * RD, CQ), 'w_kr': w(ks[7], H * RD, E), 'w_out': w(ks[8], E, E)}
    _L0_attn_in = _L0_attn_setup()

    def _L0_ffn_setup():
        import jax, jax.numpy as jnp
        import numpy as np
        B, S, HID = (2, 256, 256)
        NUM_HEADS = 16
        HEAD_DIM = HID // NUM_HEADS
        NUM_EXPERTS = 8
        TOP_K = 2
        INTER = 512
        EPS = 1e-05

        def _rmsnorm(x, w, eps=EPS):
            return x * jax.lax.rsqrt(jnp.mean(x * x, axis=-1, keepdims=True) + eps) * w

        def _moe(x_flat, Wr, Wg, Wu, Wd):
            T = x_flat.shape[0]
            logits = x_flat @ Wr.T
            top_logits, top_idx = jax.lax.top_k(logits, TOP_K)
            probs = jax.nn.softmax(top_logits, axis=-1)
            cw = jnp.zeros((T, NUM_EXPERTS), x_flat.dtype)
            cw = cw.at[jnp.arange(T)[:, None], top_idx].add(probs)
            hg = jnp.einsum('eih,th->eti', Wg, x_flat)
            hu = jnp.einsum('eih,th->eti', Wu, x_flat)
            y = jnp.einsum('ehi,eti->eth', Wd, jax.nn.silu(hg) * hu)
            return jnp.einsum('eth,te->th', y, cw)
        key = jax.random.key(seed)
        ks = jax.random.split(key, 12)
        sd_h = 1.0 / np.sqrt(HID)
        sd_i = 1.0 / np.sqrt(INTER)
        return {'x': jax.random.normal(ks[0], (B, S, HID), jnp.float32), 'Wq': jax.random.normal(ks[1], (HID, HID), jnp.float32) * sd_h, 'Wk': jax.random.normal(ks[2], (HID, HID), jnp.float32) * sd_h, 'Wv': jax.random.normal(ks[3], (HID, HID), jnp.float32) * sd_h, 'Wo': jax.random.normal(ks[4], (HID, HID), jnp.float32) * sd_h, 'w_ln1': jnp.ones((HID,), jnp.float32), 'w_ln2': jnp.ones((HID,), jnp.float32), 'Wr': jax.random.normal(ks[5], (NUM_EXPERTS, HID), jnp.float32) * sd_h, 'Wg': jax.random.normal(ks[6], (NUM_EXPERTS, INTER, HID), jnp.float32) * sd_h, 'Wu': jax.random.normal(ks[7], (NUM_EXPERTS, INTER, HID), jnp.float32) * sd_h, 'Wd': jax.random.normal(ks[8], (NUM_EXPERTS, HID, INTER), jnp.float32) * sd_i}
    _L0_ffn_in = _L0_ffn_setup()
    _d = {'L0_attn_x': _L0_attn_in['x'], 'L0_attn_w_dq': _L0_attn_in['w_dq'], 'L0_attn_w_uq': _L0_attn_in['w_uq'], 'L0_attn_w_dkv': _L0_attn_in['w_dkv'], 'L0_attn_w_uk': _L0_attn_in['w_uk'], 'L0_attn_w_uv': _L0_attn_in['w_uv'], 'L0_attn_w_qr': _L0_attn_in['w_qr'], 'L0_attn_w_kr': _L0_attn_in['w_kr'], 'L0_attn_w_out': _L0_attn_in['w_out'], 'L0_ffn_Wq': _L0_ffn_in['Wq'], 'L0_ffn_Wk': _L0_ffn_in['Wk'], 'L0_ffn_Wv': _L0_ffn_in['Wv'], 'L0_ffn_Wo': _L0_ffn_in['Wo'], 'L0_ffn_w_ln1': _L0_ffn_in['w_ln1'], 'L0_ffn_w_ln2': _L0_ffn_in['w_ln2'], 'L0_ffn_Wr': _L0_ffn_in['Wr'], 'L0_ffn_Wg': _L0_ffn_in['Wg'], 'L0_ffn_Wu': _L0_ffn_in['Wu'], 'L0_ffn_Wd': _L0_ffn_in['Wd']}
    _x0 = _d['L0_attn_x']
    _d['L0_attn_x'] = jax.random.normal(jax.random.fold_in(jax.random.key(seed), 1), (8, 256, 256), dtype=_x0.dtype)
    del _x0
    return _d

def reference(L0_attn_x, L0_attn_w_dq, L0_attn_w_uq, L0_attn_w_dkv, L0_attn_w_uk, L0_attn_w_uv, L0_attn_w_qr, L0_attn_w_kr, L0_attn_w_out, L0_ffn_Wq, L0_ffn_Wk, L0_ffn_Wv, L0_ffn_Wo, L0_ffn_w_ln1, L0_ffn_w_ln2, L0_ffn_Wr, L0_ffn_Wg, L0_ffn_Wu, L0_ffn_Wd):

    def _L0_attn_ref(x, w_dq, w_uq, w_dkv, w_uk, w_uv, w_qr, w_kr, w_out):
        import jax, jax.numpy as jnp
        import numpy as np
        E = 256
        H = 16
        HD = E // H
        CKV = 64
        CQ = 192
        RD = 64
        SCALE = 1.0 / np.sqrt(HD + RD)

        def _rope(qr, kr, offset=0):
            s = qr.shape[2]
            t = jnp.arange(offset, offset + s, dtype=jnp.float32)
            inv_freq = 1.0 / 10000.0 ** (jnp.arange(0, RD, 2, dtype=jnp.float32) / RD)
            freqs = t[:, None] * inv_freq[None, :]
            cos = jnp.concatenate([jnp.cos(freqs)] * 2, axis=-1)
            sin = jnp.concatenate([jnp.sin(freqs)] * 2, axis=-1)

            def rot(x):
                x1, x2 = (x[..., :RD // 2], x[..., RD // 2:])
                return jnp.concatenate([-x2, x1], axis=-1)
            return (qr * cos + rot(qr) * sin, kr * cos + rot(kr) * sin)
        b, s, _ = x.shape
        c_q = x @ w_dq.T
        q_c = (c_q @ w_uq.T).reshape(b, s, H, HD).transpose(0, 2, 1, 3)
        c_kv = x @ w_dkv.T
        k_c = (c_kv @ w_uk.T).reshape(b, s, H, HD).transpose(0, 2, 1, 3)
        v = (c_kv @ w_uv.T).reshape(b, s, H, HD).transpose(0, 2, 1, 3)
        q_r = (c_q @ w_qr.T).reshape(b, s, H, RD).transpose(0, 2, 1, 3)
        k_r = (x @ w_kr.T).reshape(b, s, H, RD).transpose(0, 2, 1, 3)
        q_r, k_r = _rope(q_r, k_r, offset=0)
        q = jnp.concatenate([q_c, q_r], axis=-1)
        k = jnp.concatenate([k_c, k_r], axis=-1)
        attn = jnp.einsum('bhqd,bhkd->bhqk', q, k) * SCALE
        mask = jnp.triu(jnp.full((s, s), -jnp.inf, jnp.float32), k=1)
        attn = jax.nn.softmax((attn + mask).astype(jnp.float32), axis=-1).astype(q.dtype)
        out = jnp.einsum('bhqk,bhkd->bhqd', attn, v)
        out = out.transpose(0, 2, 1, 3).reshape(b, s, H * HD)
        return out @ w_out.T

    def _L0_ffn_ref(x, Wq, Wk, Wv, Wo, w_ln1, w_ln2, Wr, Wg, Wu, Wd):
        import jax, jax.numpy as jnp
        import numpy as np
        B, S, HID = (2, 256, 256)
        NUM_HEADS = 16
        HEAD_DIM = HID // NUM_HEADS
        NUM_EXPERTS = 8
        TOP_K = 2
        INTER = 512
        EPS = 1e-05

        def _rmsnorm(x, w, eps=EPS):
            return x * jax.lax.rsqrt(jnp.mean(x * x, axis=-1, keepdims=True) + eps) * w

        def _moe(x_flat, Wr, Wg, Wu, Wd):
            T = x_flat.shape[0]
            logits = x_flat @ Wr.T
            top_logits, top_idx = jax.lax.top_k(logits, TOP_K)
            probs = jax.nn.softmax(top_logits, axis=-1)
            cw = jnp.zeros((T, NUM_EXPERTS), x_flat.dtype)
            cw = cw.at[jnp.arange(T)[:, None], top_idx].add(probs)
            hg = jnp.einsum('eih,th->eti', Wg, x_flat)
            hu = jnp.einsum('eih,th->eti', Wu, x_flat)
            y = jnp.einsum('ehi,eti->eth', Wd, jax.nn.silu(hg) * hu)
            return jnp.einsum('eth,te->th', y, cw)
        b, s, hid = x.shape
        residual = x
        xn = _rmsnorm(x, w_ln1)
        q = (xn @ Wq.T).reshape(b, s, NUM_HEADS, HEAD_DIM)
        k = (xn @ Wk.T).reshape(b, s, NUM_HEADS, HEAD_DIM)
        v = (xn @ Wv.T).reshape(b, s, NUM_HEADS, HEAD_DIM)
        scale = 1.0 / np.sqrt(HEAD_DIM)
        attn = jnp.einsum('bqhd,bkhd->bhqk', q, k) * scale
        causal = jnp.tril(jnp.ones((s, s), bool))
        attn = jnp.where(causal[None, None], attn, -jnp.inf)
        attn = jax.nn.softmax(attn, axis=-1)
        h = jnp.einsum('bhqk,bkhd->bqhd', attn, v).reshape(b, s, hid)
        x = residual + h @ Wo.T
        residual = x
        xn = _rmsnorm(x, w_ln2)
        moe_out = _moe(xn.reshape(-1, hid), Wr, Wg, Wu, Wd).reshape(b, s, hid)
        return residual + moe_out
    x = L0_attn_x
    xn = _layernorm(x, axis=-1)
    s = _L0_attn_ref(xn, L0_attn_w_dq, L0_attn_w_uq, L0_attn_w_dkv, L0_attn_w_uk, L0_attn_w_uv, L0_attn_w_qr, L0_attn_w_kr, L0_attn_w_out)
    g = _silu(_L0_ffn_ref(xn, L0_ffn_Wq, L0_ffn_Wk, L0_ffn_Wv, L0_ffn_Wo, L0_ffn_w_ln1, L0_ffn_w_ln2, L0_ffn_Wr, L0_ffn_Wg, L0_ffn_Wu, L0_ffn_Wd))
    x = x + s * g
    return x

_drawn_inputs = setup_inputs


def setup_inputs(seed=0):
    import zlib

    import numpy as np

    out = dict(_drawn_inputs(seed))
    spreads = {'L0_ffn_w_ln1': (1.0, 0.2), 'L0_ffn_w_ln2': (1.0, 0.2)}
    factors = {}
    for name, (base, spread) in spreads.items():
        noise = np.random.default_rng([zlib.crc32(name.encode()), seed]).standard_normal(out[name].shape)
        drawn = base * np.exp(spread * noise) if base else spread * noise
        out[name] = jnp.asarray(drawn.astype(out[name].dtype))
    for name, factor in factors.items():
        out[name] = (out[name] * factor).astype(out[name].dtype)
    return out
```

```python
from contextlib import ExitStack

import numpy as np

import concourse.bass as bass
from concourse import mybir

F32 = mybir.dt.float32
F32R = mybir.dt.float32r
BF16 = mybir.dt.bfloat16
U32 = mybir.dt.uint32
ALU = mybir.AluOpType
ACT = mybir.ActivationFunctionType
AX = mybir.AxisListType

P = 128
B, S, E = 8, 256, 256
H, D, RD = 16, 16, 64
CQ, CKV = 192, 64
NE, FF = 8, 512
T = B * S
TT = T // P
ET = E // P
HW = RD + D
HS = 96
MROW = HW
G = 4
NG = H // G
PADV = 32
ST = 64
MROW2 = 3 * D
QC, KC, VC = 0, H * HW, 2 * H * HW
Q2C = VC + H * D
V2C = Q2C + 2 * H * D
WC = V2C + H * D
CH = G * HW
EPS = 1e-5
BIG = -1e30
IT = FF // P
TC = 512
NC = T // TC
WG, WU, WD = 0, ET * FF, 2 * ET * FF
WE = WD + IT * E


def build(nc, x, w_cols, w_dq, w_uqr, w_dkv, w_ukv, w_out, w_o, w_ln1, w_ln2, w_r, w_experts,
          cosines, sines, ident, mask, mask_t, experts_iota, out):
    ctx = ExitStack()
    with ctx:
        def sb(name, shape, dt=F32, stack=ctx):
            return stack.enter_context(nc.sbuf_tensor(name, shape, dt))

        def sem(name):
            return ctx.enter_context(nc.semaphore(name))

        xn = sb("xn", [P, TT, E])
        s_tok = sb("s_tok", [P, TT, E])
        idf = sb("idf", [P, P])
        ln2 = sb("ln2", [P, ET])
        wr = sb("wr", [P, ET, NE])
        rms1 = sb("rms1", [P, TT])
        mv = sb("mv", [P, TT, 2])
        stats = sb("stats", [P, TT, 6])
        msq = sb("msq", [P, TT])
        rstd = sb("rstd", [P, TT])
        mhalf = sb("mhalf", [P, TT])

        att = ExitStack()
        cos_t = sb("cos_t", [P, ET, HW], F32, att)
        sin_t = sb("sin_t", [P, ET, RD], F32, att)
        idb = sb("idb", [P, P], BF16, att)
        maskb = sb("maskb", [P, 2, P], BF16, att)
        wh = sb("wh", [P, ET, WC], F32R, att)
        wl = sb("wl", [P, ET, WC], F32R, att)
        wo1 = sb("wo1", [P, NG, E], F32, att)
        wo2 = sb("wo2", [P, NG, E], F32, att)
        ln1 = sb("ln1", [P, ET], F32, att)
        xb = sb("xb", [P, 2, E], F32, att)
        rb = sb("rb", [P, 2], F32, att)
        xth = sb("xth", [P, ET, S], F32R, att)
        xtl = sb("xtl", [P, ET, S], F32R, att)
        tok = sb("tok", [P, 4, G, HS], F32, att)
        swp = sb("swp", [P, 2, G, RD], F32, att)
        qr = sb("qr", [HS, 2, 2, S], F32R, att)
        kr = sb("kr", [HS, 2, 2, S], F32R, att)
        y2 = sb("y2", [P, 2, H, D], F32, att)
        qs = sb("qs", [P, H, ST], F32R, att)
        ks = sb("ks", [P, H, ST], F32R, att)
        qt2 = sb("qt2", [P, H // 2, S], F32R, att)
        kt2 = sb("kt2", [P, H // 2, S], F32R, att)
        v1 = sb("v1", [P, 2, H, PADV], F32, att)
        v2 = sb("v2", [P, 2, H, PADV], F32, att)
        ones = sb("ones", [P, PADV], F32, att)
        ex = sb("ex", [P, 2 * G, 3 * P], F32, att)
        ot = sb("ot", [P, NG, S], F32, att)
        rec = sb("rec", [P, S], F32, att)
        negm1 = sb("negm1", [P, 2, H], F32, att)
        negm2 = sb("negm2", [P, 2, H], F32, att)
        mt1 = sb("mt1", [H, S], F32, att)
        mt2 = sb("mt2", [H, S], F32R, att)
        prep = ExitStack()
        mask_f = sb("mask_f", [P, 2, P], F32, prep)
        w_cols_raw = sb("w_cols_raw", [P, ET, H * RD + 3 * E], F32, prep)
        w_uqr_raw = sb("w_uqr_raw", [P, 2, H * HW], F32, prep)
        w_dq_raw = sb("w_dq_raw", [P, 2, E], F32, prep)
        w_dkv_raw = sb("w_dkv_raw", [CKV, E], F32, prep)
        w_ukv_raw = sb("w_ukv_raw", [CKV, 2 * H * D], F32, prep)
        prep.close()
        qt = sb("qt", [HS, H, S], F32, att)
        kt = sb("kt", [HS, H, S], F32, att)
        att.close()

        moe = ExitStack()
        raw = sb("raw", [P, 2, WE], F32, moe)
        weh = sb("weh", [P, 2, WE], F32R, moe)
        wel = sb("wel", [P, 2, WE], F32R, moe)
        x2h = sb("x2h", [P, ET, T], F32R, moe)
        x2l = sb("x2l", [P, ET, T], F32R, moe)
        xb2 = sb("xb2", [P, 2, E], F32, moe)
        yt = sb("yt", [P, 2, ET, P], F32, moe)
        lg = sb("lg", [P, TT, NE], F32, moe)
        mx = sb("mx", [P, TT, NE], F32, moe)
        ix = sb("ix", [P, TT, NE], U32, moe)
        ixf = sb("ixf", [P, TT, 2], F32, moe)
        iot = sb("iot", [P, TT, NE], F32, moe)
        gate = sb("gate", [P, 4, TT], F32, moe)
        pick = sb("pick", [P, 2, TT, NE], F32, moe)
        cw = sb("cw", [P, NE, TT], F32, moe)
        sg = sb("sg", [P, 2, TC], F32, moe)
        hf = sb("hf", [P, 2, TC], F32, moe)
        hh = sb("hh", [P, 2, TC], F32R, moe)
        hl = sb("hl", [P, 2, TC], F32R, moe)
        xr = sb("xr", [P, TT, E], F32, moe)
        gl = sb("gl", [P, 4, E], F32, moe)
        moe.close()

        ps = [ctx.enter_context(nc.psum_tensor(f"ps{i}", [P, 512], F32)) for i in range(8)]

        s_w = sem("weights_loaded")
        s_c = sem("constants_loaded")
        s_x = sem("x_loaded")
        cast = sem("masks_cast")
        clear = sem("pads_set")
        comb = sem("weights_combined")
        combh = sem("combined_high")
        combl = sem("combined_low")
        wfh = sem("direct_high")
        wdone = sem("direct_low")
        wln = sem("mha_weights_scaled")
        st_a = sem("stats_taken")
        st_b = sem("stats_joined")
        powd = sem("rstd_ready")
        xnd = sem("xn_ready")
        msd = sem("mean_squares")
        rmd = sem("rms1_ready")
        xbd = sem("batch_copied")
        tr0 = sem("xT_transposed")
        xthd = sem("xT_high")
        xtld = sem("xT_low")
        p1d = sem("mla_projected")
        roped = sem("rope_products")
        tokd = sem("rope_done")
        tr1 = sem("mla_transposed")
        qke = sem("mla_qk_kept")
        v1d = sem("mla_v_kept")
        rrd = sem("mla_qk_rounded")
        m1d = sem("mla_scores")
        mx1 = sem("mla_max")
        mtr1 = sem("mla_max_transposed")
        mte1 = sem("mla_max_kept")
        md1 = sem("mla_max_row")
        st1 = sem("mla_scores_t")
        ex1 = sem("mla_exp")
        pv1 = sem("mla_pv")
        rc1 = sem("mla_reciprocal")
        ot1 = sem("mla_heads")
        o1 = sem("mla_out")
        sd = sem("mla_out_kept")
        p2d = sem("mha_projected")
        y2d = sem("mha_qk_scaled")
        v2d = sem("mha_v_kept")
        hi2 = sem("mha_qk_high")
        s2d = sem("mha_qk_stacked")
        tr2 = sem("mha_transposed")
        t2e = sem("mha_qk_kept")
        m2d = sem("mha_scores")
        mx2 = sem("mha_max")
        mtr2 = sem("mha_max_transposed")
        mte2 = sem("mha_max_kept")
        md2 = sem("mha_max_row")
        st2 = sem("mha_scores_t")
        ex2 = sem("mha_exp")
        pv2 = sem("mha_pv")
        rc2 = sem("mha_reciprocal")
        ot2 = sem("mha_heads")
        o2 = sem("mha_out")
        x2d = sem("ffn_residual")
        st_c = sem("stats2_taken")
        st_d = sem("stats2_joined")
        ms2 = sem("mean_squares2")
        rm2 = sem("rms2_ready")
        xb2d = sem("x2_scaled")
        tr3 = sem("x2_transposed")
        ytd = sem("x2T_scaled")
        x2hd = sem("x2T_high")
        x2ld = sem("x2T_low")
        lgd = sem("router_logits")
        lgk = sem("logits_kept")
        top = sem("top2_found")
        gch = sem("gate_steps")
        gex = sem("gate_exp")
        cwd = sem("expert_weights_ready")
        rawd = [sem("expert_loaded_even"), sem("expert_loaded_odd")]
        wehd = sem("expert_high")
        weld = sem("expert_low")
        gd = sem("hg_done")
        ud = sem("hu_done")
        sgd = sem("silu_done")
        hfd = sem("h_done")
        hhd = sem("h_high")
        hld = sem("h_low")
        dd = sem("down_done")
        yd = sem("y_added")
        xrd = sem("x_again")
        gld = sem("ffn_silu")
        mud = sem("branches_multiplied")
        fin = sem("result_ready")
        s_out = sem("stored")

        last = B - 1
        N_DIRECT = 2 * ET
        N_COMB = ET * (NG + 1)

        block = ctx.enter_context(nc.Block())

        @block.sync
        def _(sp):
            sp.dma_start(xn[:, :, :], x.rearrange("(t p) e -> p t e", p=P)).then_inc(s_x, 16)
            for dst, src in ((w_dq_raw[0:P, 0, :], w_dq[0:P, :]), (w_dq_raw[0:CQ - P, 1, :], w_dq[P:CQ, :]),
                             (w_uqr_raw[0:P, 0, :], w_uqr[0:P, :]), (w_uqr_raw[0:CQ - P, 1, :], w_uqr[P:CQ, :]),
                             (w_dkv_raw[:, :], w_dkv), (w_ukv_raw[:, :], w_ukv),
                             (w_cols_raw[:, :, :], w_cols.rearrange("(m p) n -> p m n", p=P)),
                             (ln1[:, :], w_ln1)):
                sp.dma_start(dst, src).then_inc(s_w, 16)
            for dst, src in ((idf[:, :], ident), (cos_t[:, :, :], cosines), (sin_t[:, :, :], sines),
                             (mask_f[:, 0, :], mask), (mask_f[:, 1, :], mask_t), (ln2[:, :], w_ln2),
                             (wr[:, :, :], w_r.rearrange("(m p) n -> p m n", p=P)),
                             (wo1[:, :, :], w_out.rearrange("(g p) e -> p g e", p=P)),
                             (wo2[:, :, :], w_o.rearrange("(g p) e -> p g e", p=P))):
                sp.dma_start(dst, src).then_inc(s_c, 16)

            with sp.Fori(0, B) as b:
                sp.wait_ge(mte1, b + 1)
                sp.dma_start(qt[MROW:MROW + 1, :, :], mt1[:, :]).then_inc(md1, 16)
                sp.wait_ge(mte2, b + 1)
                for e in range(2):
                    r = ST * e + MROW2
                    sp.dma_start(qt2[r:r + 1, :, :].bitcast(F32),
                                 mt2[e * H // 2:(e + 1) * H // 2, :].bitcast(F32)).then_inc(md2, 16)

            sp.wait_ge(x2d, TT)
            def load(e, s):
                sp.dma_start(raw[:, s, :], w_experts[e, :, :]).then_inc(rawd[s], 16)
            load(0, 0)
            load(1, 1)
            sp.dma_start(iot[:, :, :], experts_iota).then_inc(xrd, 16)
            sp.dma_start(xr[:, :, :], x.rearrange("(t p) e -> p t e", p=P)).then_inc(xrd, 16)
            with sp.Fori(0, NE // 2 - 1) as i:
                for s in range(2):
                    sp.wait_ge(weld, 2 * i + s + 1)
                    sp.dma_start(raw[:, s, :],
                                 w_experts[bass.ds(2 * i + s + 2, 1), :, :].rearrange("o p n -> (o p) n")
                                 ).then_inc(rawd[s], 16)
            o_v = out.rearrange("(t p) e -> p t e", p=P)
            for j in range(TT // 4):
                sp.wait_ge(fin, j + 1)
                sp.dma_start(o_v[:, 4 * j:4 * j + 4, :], xr[:, 4 * j:4 * j + 4, :]).then_inc(s_out, 16)
            sp.wait_ge(s_out, 16 * (TT // 4))

        @block.gpsimd
        def _(pool):
            nc.gpsimd.memset(mhalf[:, :], -0.5).then_inc(clear, 1)
            pool.wait_ge(clear, 1)
            pool.wait_ge(st_b, TT + 1)
            nc.gpsimd.tensor_tensor(rstd[:, :], msq[:, :], mhalf[:, :], ALU.pow).then_inc(powd, 1)
            pool.wait_ge(msd, TT + 2)
            nc.gpsimd.tensor_tensor(rms1[:, :], msq[:, :], mhalf[:, :], ALU.pow).then_inc(rmd, 1)

            with pool.Fori(0, B) as b:
                for n in range(2 * 2 * NG):
                    pool.wait_ge(roped, 16 * b + n + 1)
                    t = tok[:, n % 4, :, 0:RD]
                    nc.gpsimd.tensor_tensor(t, t, swp[:, n % 2, :, :], ALU.add).then_inc(tokd, 1)

            pool.wait_ge(ms2, 2)
            nc.gpsimd.tensor_tensor(rstd[:, :], msq[:, :], mhalf[:, :], ALU.pow).then_inc(rm2, 1)

        def order(step_proj, step_tr):
            for i in range(2 * 9 + 2):
                if i < 18:
                    step_proj(i)
                if i >= 2 and (i - 2) % 9 != 8:
                    step_tr(i - 2, 8 * ((i - 2) // 9) + (i - 2) % 9)

        @block.tensor
        def _(pe):
            def mm(o, a, m, start, stop, **k):
                return nc.tensor.matmul(o, a, m, start=start, stop=stop, skip_group_check=True, **k)

            pe.wait_ge(s_w, 16 * 8)
            w = 0
            for m in range(ET):
                cols = slice(m * P, (m + 1) * P)
                for c in range(NG + 1):
                    if w >= 2:
                        pe.wait_ge(combl, w - 1)
                    if c < NG:
                        o = ps[w % 2][:, 0:CH]
                        mm(o, w_dq_raw[:, 0, cols], w_uqr_raw[:, 0, c * CH:(c + 1) * CH], True, False)
                        i = mm(o, w_dq_raw[0:CQ - P, 1, cols], w_uqr_raw[0:CQ - P, 1, c * CH:(c + 1) * CH],
                               False, True)
                    else:
                        i = mm(ps[w % 2][:, :], w_dkv_raw[:, cols], w_ukv_raw[:, :], True, True)
                    i.then_inc(comb, 1)
                    w += 1

            def proj(o, c0, n, tt):
                t = slice(tt * P, (tt + 1) * P)
                k = 0
                for a, m in ((xth, wh), (xth, wl), (xtl, wh)):
                    for e in range(ET):
                        i = mm(o, a[:, e, t], m[:, e, c0:c0 + n], k == 0, k == 2 * 3 - 1)
                        k += 1
                return i

            def stage_xt(b):
                pe.wait_ge(xbd, b + 1)
                pe.wait_ge(t2e, 8 * b)
                for e in range(ET):
                    for tt in range(2):
                        i = nc.tensor.transpose(ps[2][:, (2 * e + tt) * P:(2 * e + tt + 1) * P],
                                                xb[:, tt, e * P:(e + 1) * P], idf[:, :])
                i.then_inc(tr0, 1)

            def stage_p1(b):
                pe.wait_ge(xtld, b + 1)
                pe.wait_ge(sd, 2 * b)

                def step_proj(i):
                    tt, c = i // 9, i % 9
                    if i >= 2:
                        j = i - 2
                        if j % 9 == 8:
                            pe.wait_ge(v1d, 2 * b + j // 9 + 1)
                        else:
                            pe.wait_ge(roped, 16 * b + 8 * (j // 9) + j % 9 + 1)
                    if c < 8:
                        c0 = (QC, KC)[c % 2] + (c // 2) * CH
                        proj(ps[i % 2][:, 0:CH], c0, CH, tt).then_inc(p1d, 1)
                    else:
                        proj(ps[i % 2][:, 0:H * D], VC, H * D, tt).then_inc(p1d, 1)

                def step_tr(i, n):
                    pe.wait_ge(tokd, 16 * b + n + 1)
                    if n >= 2:
                        pe.wait_ge(qke, 16 * b + n - 1)
                    for j in range(G):
                        t = nc.tensor.transpose(ps[2 + n % 2][0:HS, j * P:(j + 1) * P], tok[:, n % 4, j, :],
                                                idf[:, :])
                    t.then_inc(tr1, 1)

                order(step_proj, step_tr)

            def stage_m1(b):
                pe.wait_ge(ex2, 16 * b)
                for h in range(H):
                    g, j = h // 2, h % 2
                    if j == 0:
                        pe.wait_ge(rrd, H // 2 * b + g + 1)
                    if h >= 2:
                        pe.wait_ge(mx1, 16 * b + h - 1)
                    o = ps[4 + h % 2]
                    for t in range(2):
                        mm(o[:, t * S:(t + 1) * S], qr[:, g % 2, j, t * P:(t + 1) * P], kr[:, g % 2, j, :], True, False)
                        i = mm(o[:, 3 * P * t:3 * P * t + P], idb[:, :], maskb[:, 0, :], False, True)
                    i.then_inc(m1d, 1)

            def max_t(b, negm, mx, mtr):
                pe.wait_ge(mx, 16 * b + H)
                for t in range(2):
                    i = nc.tensor.transpose(ps[4][0:H, t * P:(t + 1) * P], negm[:, t, :], idf[:, :])
                i.then_inc(mtr, 1)

            def stage_p2(b):
                pe.wait_ge(x2d, 2 * b)
                pe.wait_ge(roped, 16 * b + 16)
                pe.wait_ge(v1d, 2 * b + 2)
                for j in range(4):
                    tt = j // 2
                    if j >= 2:
                        pe.wait_ge((y2d, v2d)[j % 2], 2 * b + 1)
                    if j % 2 == 0:
                        proj(ps[0][:, :], Q2C, 2 * H * D, tt).then_inc(p2d, 1)
                    else:
                        proj(ps[1][:, 0:H * D], V2C, H * D, tt).then_inc(p2d, 1)
                max_t(b, negm1, mx1, mtr1)
                pe.wait_ge(qke, 16 * b + 16)
                for u in range(8):
                    if u % 4 == 0:
                        pe.wait_ge(s2d, 2 * b + u // 4 + 1)
                    if u >= 2:
                        pe.wait_ge(t2e, 8 * b + u - 1)
                    a = (qs, ks)[u % 4 // 2][:, :, :].rearrange("p h c -> p (h c)").bitcast(F32)
                    for j in range(4):
                        p0 = (4 * (u % 2) + j) * P
                        i = nc.tensor.transpose(ps[2 + u % 2][:, j * P:(j + 1) * P], a[:, p0:p0 + P], idf[:, :])
                    i.then_inc(tr2, 1)

            def stage_m2(b):
                pe.wait_ge(t2e, 8 * b + 8)
                pe.wait_ge(ex1, 16 * b + 16)
                for h in range(H):
                    r, p = ST * (h % 2), h // 2
                    if h >= 2:
                        pe.wait_ge(mx2, 16 * b + h - 1)
                    o = ps[4 + h % 2]
                    for t in range(2):
                        mm(o[:, t * S:(t + 1) * S], qt2[r:r + MROW2, p, t * P:(t + 1) * P],
                           kt2[r:r + MROW2, p, :], True, False)
                        i = mm(o[:, 3 * P * t:3 * P * t + P], idb[:, :], maskb[:, 0, :], False, True)
                    i.then_inc(m2d, 1)

            def heads(b, scores_t, st, ex_, pv, v, before_h0, before_pv0, ot_):
                before_h0()

                def values(g):
                    pe.wait_ge(ex_, 16 * b + G * (g + 1))
                    if g == 0:
                        before_pv0()
                    else:
                        pe.wait_ge(ot_, NG * b + g)
                    for k, (o0, e0, n) in enumerate(((0, P, S), (P, 0, P))):
                        for bank, lhs in ((6, v), (7, None)):
                            for j in range(G):
                                h = G * g + j
                                a = ones[:, :] if lhs is None else lhs[:, k, h, :]
                                i = mm(ps[bank][PADV * j:PADV * (j + 1), o0:o0 + n], a,
                                       ex[:, h % (2 * G), e0:e0 + n], k == 0, k == 1,
                                       tile_position=(0, PADV * j))
                    i.then_inc(pv, 1)

                for g in range(NG):
                    for j in range(G):
                        h = G * g + j
                        if h >= 2:
                            pe.wait_ge(ex_, 16 * b + h - 1)
                        scores_t(h, ps[4 + h % 2]).then_inc(st, 1)
                    if g:
                        values(g - 1)
                values(NG - 1)

            def project_heads(b, ot_, wo, od, before):
                before()
                pe.wait_ge(ot_, NG * b + NG)
                for tt in range(2):
                    for g in range(NG):
                        i = mm(ps[tt][:, 0:E], ot[:, g, tt * P:(tt + 1) * P], wo[:, g, :], g == 0, g == NG - 1)
                    i.then_inc(od, 1)

            def scores1(h, o):
                mm(o[:, P:2 * P], kt[:, h, P:S], qt[:, h, P:S], True, False)
                mm(o[:, P:2 * P], idb[:, :], maskb[:, 1, :], False, True)
                mm(o[:, 2 * P:4 * P], kt[:, h, 0:P], qt[:, h, :], True, False)
                return mm(o[:, 2 * P:3 * P], idb[:, :], maskb[:, 1, :], False, True)

            def scores2(h, o):
                r, p = ST * (h % 2), h // 2
                mm(o[:, 0:2 * P], kt2[r:r + ST, p, P:S], qt2[r:r + ST, p, :], True, False)
                mm(o[:, P:2 * P], idb[:, :], maskb[:, 1, :], False, True)
                mm(o[:, 2 * P:4 * P], kt2[r:r + ST, p, 0:P], qt2[r:r + ST, p, :], True, False)
                return mm(o[:, 2 * P:3 * P], idb[:, :], maskb[:, 1, :], False, True)

            def stage_t1(b):
                def before_h0():
                    pe.wait_ge(mte1, b + 1)
                    pe.wait_ge(md1, 16 * b + 16)
                    pe.wait_ge(v1d, 2 * b + 2)
                heads(b, scores1, st1, ex1, pv1, v1, before_h0, lambda: pe.wait_ge(ot2, NG * b), ot1)
                project_heads(b, ot1, wo1, o1, lambda: (pe.wait_ge(y2d, 2 * b + 2), pe.wait_ge(v2d, 2 * b + 2)))

            def stage_t2(b, more):
                def before_h0():
                    pe.wait_ge(mte2, b + 1)
                    pe.wait_ge(md2, 32 * b + 32)
                    pe.wait_ge(v2d, 2 * b + 2)
                heads(b, scores2, st2, ex2, pv2, v2, before_h0, lambda: pe.wait_ge(ot1, NG * b + NG), ot2)
                if more:
                    project_heads(b, ot2, wo2, o2,
                                  lambda: (pe.wait_ge(roped, 16 * b + 32), pe.wait_ge(v1d, 2 * b + 4)))
                else:
                    project_heads(b, ot2, wo2, o2, lambda: pe.wait_ge(sd, 2 * b + 2))

            pe.wait_ge(s_c, 16 * 9)
            pe.wait_ge(cast, 2)
            pe.wait_ge(clear, 6)
            pe.wait_ge(combl, N_COMB)
            pe.wait_ge(wdone, N_DIRECT)

            def batch(b, more):
                stage_m1(b)
                stage_p2(b)
                stage_t1(b)
                stage_m2(b)
                if more:
                    stage_xt(b + 1)
                max_t(b, negm2, mx2, mtr2)
                if more:
                    stage_p1(b + 1)
                stage_t2(b, more)

            stage_xt(0)
            stage_p1(0)
            with pe.Fori(0, last) as b:
                batch(b, True)
            batch(last, False)

            pe.wait_ge(x2d, TT)
            pe.wait_ge(ex2, 16 * B)
            with pe.Fori(0, TT // 2) as i:
                for s in range(2):
                    pe.wait_ge(xb2d, 2 * i + s + 1)
                    pe.wait_ge(ytd, 2 * i)
                    for e in range(ET):
                        t = nc.tensor.transpose(ps[s][:, e * P:(e + 1) * P], xb2[:, s, e * P:(e + 1) * P], idf[:, :])
                    t.then_inc(tr3, 1)
                for s in range(2):
                    pe.wait_ge(ytd, 2 * i + s + 1)
                    pe.wait_ge(lgk, 2 * i)
                    for e in range(ET):
                        t = mm(ps[2 + s][:, 0:NE], yt[:, s, e, :], wr[:, e, :], e == 0, e == ET - 1)
                    t.then_inc(lgd, 1)

            def gate_up(e, s, c, it):
                n = 16 * e + 4 * c + it
                pe.wait_ge(weld, e + 1)
                for w0, bank, done, free in ((WG, 0, gd, sgd), (WU, 2, ud, hfd)):
                    if it >= 2:
                        pe.wait_ge(free, n - 1)
                    else:
                        pe.wait_ge(free, n if isinstance(n, int) and n < 2 else n - 1)
                    k = 0
                    for wt, xt in ((weh, x2h), (wel, x2h), (weh, x2l)):
                        for m in range(ET):
                            a = wt[:, s, w0 + m * FF + it * P:w0 + m * FF + (it + 1) * P]
                            i = mm(ps[bank + it % 2][:, :], a, xt[:, m, bass.ds(c * TC, TC)], k == 0, k == 5)
                            k += 1
                    i.then_inc(done, 1)

            def down(e, s, c, it):
                n = 16 * e + 4 * c + it
                pe.wait_ge(hld, n + 1)
                if it == 0:
                    pe.wait_ge(yd, 4 * e + c)
                for t in range(TC // P):
                    o = ps[4 + t // 2][:, (t % 2) * E:(t % 2 + 1) * E]
                    for k, (a, m) in enumerate(((hh, weh), (hh, wel), (hl, weh))):
                        i = mm(o, a[:, it % 2, t * P:(t + 1) * P], m[:, s, WD + it * E:WD + (it + 1) * E],
                               it == 0 and k == 0 and t % 2 == 0, it == IT - 1 and k == 2)
                i.then_inc(dd, 1)

            def expert(e, s, final):
                def chunk(c, nxt):
                    for it in range(1, IT):
                        gate_up(e, s, c, it)
                        down(e, s, c, it - 1)
                    nxt()
                    down(e, s, c, IT - 1)
                with pe.Fori(0, NC - 1) as c:
                    chunk(c, lambda: gate_up(e, s, c + 1, 0))
                chunk(NC - 1, (lambda: None) if final else (lambda: gate_up(e + 1, 1 - s, 0, 0)))

            pe.wait_ge(x2ld, TT)
            pe.wait_ge(lgk, TT)
            gate_up(0, 0, 0, 0)
            with pe.Fori(0, NE // 2 - 1) as i:
                for s in range(2):
                    expert(2 * i + s, s, False)
            expert(NE - 2, 0, False)
            expert(NE - 1, 1, True)

        @block.scalar
        def _(act):
            def copy(o, a):
                return nc.scalar.activation(o, a, ACT.Copy)

            w = 0
            for m in range(ET):
                for c in range(NG + 1):
                    act.wait_ge(comb, w + 1)
                    o = ps[w % 2]
                    if c < NG:
                        copy(wh[:, m, QC + c * CH:QC + (c + 1) * CH], o[:, 0:CH]).then_inc(combh, 1)
                    else:
                        copy(wh[:, m, KC:VC].rearrange("p (h c) -> p h c", h=H)[:, :, RD:HW],
                             o[:, 0:H * D].rearrange("p (h c) -> p h c", h=H))
                        copy(wh[:, m, VC:VC + H * D], o[:, H * D:2 * H * D]).then_inc(combh, 1)
                    w += 1

            def stage_xt(b):
                act.wait_ge(tr0, b + 1)
                act.wait_ge(p2d, 4 * b)
                copy(xth[:, :, :].rearrange("p e t -> p (e t)"), ps[2][:, :]).then_inc(xthd, 1)

            def stage_p1(b):
                act.wait_ge(st1, 16 * b)
                act.wait_ge(pv1, NG * b)

                def step_proj(i):
                    if i % 9 == 8:
                        act.wait_ge(p1d, 18 * b + i + 1)
                        copy(v1[:, i // 9, :, 0:D],
                             ps[i % 2][:, 0:H * D].rearrange("p (h c) -> p h c", h=H)).then_inc(v1d, 1)

                def step_tr(i, n):
                    act.wait_ge(tr1, 16 * b + n + 1)
                    g, tt = n % 8 // 2, n // 8
                    copy((qt, kt)[n % 2][:, G * g:G * (g + 1), tt * P:(tt + 1) * P],
                         ps[2 + n % 2][0:HS, :].rearrange("p (h t) -> p h t", h=G)).then_inc(qke, 1)

                order(step_proj, step_tr)

            def max_t(b, mt, mtr, md, mte, k):
                act.wait_ge(mtr, b + 1)
                act.wait_ge(md, k * b)
                copy(mt[:, :], ps[4][0:H, 0:S]).then_inc(mte, 1)

            def stage_p2(b):
                act.wait_ge(pv2, NG * b)
                for tt in range(2):
                    r = rb[:, tt:tt + 1]
                    act.wait_ge(p2d, 4 * b + 2 * tt + 1)
                    act.wait_ge(s2d, 2 * b + tt)
                    nc.scalar.activation(y2[:, :, :, :].rearrange("p a h c -> p (a h c)"), ps[0][:, :],
                                         ACT.Copy, scale=r).then_inc(y2d, 1)
                    act.wait_ge(p2d, 4 * b + 2 * tt + 2)
                    nc.scalar.activation(v2[:, tt, :, 0:D], ps[1][:, 0:H * D].rearrange("p (h c) -> p h c", h=H),
                                         ACT.Copy, scale=r).then_inc(v2d, 1)
                max_t(b, mt1, mtr1, md1, mte1, 16)
                act.wait_ge(st2, 16 * b)
                for u in range(8):
                    act.wait_ge(tr2, 8 * b + u + 1)
                    tt = u // 4
                    copy((qt2, kt2)[u % 4 // 2][:, 4 * (u % 2):4 * (u % 2) + 4, tt * P:(tt + 1) * P],
                         ps[2 + u % 2][:, :].rearrange("p (h t) -> p h t", h=4)).then_inc(t2e, 1)

            def exps(b, st, ex_, pv, first, scale):
                first()
                for h in range(H):
                    g = h // G
                    act.wait_ge(st, 16 * b + h + 1)
                    if h % G == 0 and g >= 2:
                        act.wait_ge(pv, NG * b + g - 1)
                    nc.scalar.activation(ex[:, h % (2 * G), :], ps[4 + h % 2][:, P:4 * P], ACT.Exp,
                                         scale=scale).then_inc(ex_, 1)

            act.wait_ge(clear, 6)
            act.wait_ge(rmd, 1)
            act.wait_ge(wdone, N_DIRECT)
            act.wait_ge(combl, N_COMB)

            def batch(b, more):
                stage_p2(b)
                exps(b, st1, ex1, pv1, lambda: act.wait_ge(pv2, NG * b), float(HW) ** -0.5)
                if more:
                    stage_xt(b + 1)
                max_t(b, mt2, mtr2, md2, mte2, 32)
                if more:
                    stage_p1(b + 1)
                exps(b, st2, ex2, pv2, lambda: act.wait_ge(pv1, NG * b + NG), float(D) ** -0.5)

            stage_xt(0)
            stage_p1(0)
            with act.Fori(0, last) as b:
                batch(b, True)
            batch(last, False)

            with act.Fori(0, TT // 2) as i:
                for s in range(2):
                    act.wait_ge(tr3, 2 * i + s + 1)
                    act.wait_ge(lgd, 2 * i)
                    act.wait_ge(x2ld, 2 * i)
                    for e in range(ET):
                        a = nc.scalar.activation(yt[:, s, e, :], ps[s][:, e * P:(e + 1) * P], ACT.Copy,
                                                 scale=ln2[:, e:e + 1])
                    a.then_inc(ytd, 1)
            act.wait_ge(gch, 1)
            nc.scalar.activation(gate[:, 1, :], gate[:, 0, :], ACT.Exp).then_inc(gex, 1)

            with act.Fori(0, NE * NC) as n:
                for it in range(IT):
                    act.wait_ge(gd, 4 * n + it + 1)
                    act.wait_ge(hfd, 4 * n + max(it - 1, 0))
                    nc.scalar.activation(sg[:, it % 2, :], ps[it % 2][:, :], ACT.Silu).then_inc(sgd, 1)

            for j in range(TT // 4):
                act.wait_ge(yd, NE * NC - (TT // 4) + j + 1)
                act.wait_ge(mud, j)
                nc.scalar.activation(gl[:, :, :], xn[:, 4 * j:4 * j + 4, :], ACT.Silu).then_inc(gld, 1)

        @block.vector
        def _(dve):
            def copy(o, a):
                return nc.vector.tensor_copy(o, a)

            def minus(o, a, b):
                return nc.vector.tensor_tensor(o, a, b.bitcast(F32), ALU.subtract)

            nc.vector.memset(tok[:, :, :, RD:HS], 0.0).then_inc(clear, 1)
            nc.vector.memset(qs[:, :, :].bitcast(F32), 0.0).then_inc(clear, 1)
            nc.vector.memset(ks[:, :, :].bitcast(F32), 0.0).then_inc(clear, 1)
            nc.vector.memset(v1[:, :, :, :], 0.0)
            nc.vector.memset(v2[:, :, :, :], 0.0)
            nc.vector.memset(ones[:, :], 1.0).then_inc(clear, 1)
            dve.wait_ge(clear, 5)
            nc.vector.memset(tok[:, 1:4:2, :, MROW:MROW + 1], 1.0)
            nc.vector.memset(ks[:, :, MROW2:MROW2 + 1].bitcast(F32), 1.0).then_inc(clear, 1)
            dve.wait_ge(s_c, 16 * 9)
            copy(idb[:, :], idf[:, :]).then_inc(cast, 1)
            copy(maskb[:, :, :], mask_f[:, :, :]).then_inc(cast, 1)

            def norm_stats(done_a, done_b, first):
                with dve.Fori(0, TT) as t:
                    nc.vector.bn_stats(stats[:, bass.ds(t, 1), :].rearrange("p o c -> p (o c)"),
                                       xn[:, bass.ds(t, 1), :].rearrange("p o e -> p (o e)")).then_inc(done_a, 1)
                dve.wait_ge(done_a, TT + first)
                for t in range(TT):
                    nc.vector.bn_aggr(mv[:, t, :], stats[:, t, :]).then_inc(done_b, 1)

            dve.wait_ge(s_x, 16)
            norm_stats(st_a, st_b, 0)
            dve.wait_ge(st_b, TT)
            nc.vector.tensor_scalar(msq[:, :], mv[:, :, 1], EPS, None, ALU.add).then_inc(st_b, 1)
            dve.wait_ge(powd, 1)
            with dve.Fori(0, TT) as t:
                a = xn[:, bass.ds(t, 1), :].rearrange("p o e -> p (o e)")
                nc.vector.tensor_scalar(a, a, mv[:, bass.ds(t, 1), 0], rstd[:, bass.ds(t, 1)],
                                        ALU.subtract, ALU.mult).then_inc(xnd, 1)

            def mean_squares(done, n):
                dve.wait_ge(done, n)
                nc.vector.tensor_tensor(msq[:, :], mv[:, :, 0], mv[:, :, 0], ALU.mult).then_inc(done, 1)
                dve.wait_ge(done, n + 1)
                nc.vector.scalar_tensor_tensor(out=msq[:, :], in0=msq[:, :], scalar=EPS, in1=mv[:, :, 1],
                                               op0=ALU.add, op1=ALU.add).then_inc(done, 1)

            dve.wait_ge(xnd, TT)
            norm_stats(st_a, msd, TT)
            mean_squares(msd, TT)

            w = 0
            for m in range(ET):
                for c in range(NG + 1):
                    dve.wait_ge(combh, w + 1)
                    o = ps[w % 2]
                    if c < NG:
                        cs = slice(QC + c * CH, QC + (c + 1) * CH)
                        minus(wl[:, m, cs], o[:, 0:CH], wh[:, m, cs]).then_inc(combl, 1)
                    else:
                        kh, kl = (a[:, m, KC:VC].rearrange("p (h c) -> p h c", h=H)[:, :, RD:HW] for a in (wh, wl))
                        minus(kl, o[:, 0:H * D].rearrange("p (h c) -> p h c", h=H), kh)
                        cs = slice(VC, VC + H * D)
                        minus(wl[:, m, cs], o[:, H * D:2 * H * D], wh[:, m, cs]).then_inc(combl, 1)
                    w += 1
            dve.wait_ge(s_w, 16 * 8)
            for m in range(ET):
                a = w_cols_raw[:, m, H * RD:]
                nc.vector.tensor_scalar(a, a, ln1[:, m:m + 1], None, ALU.mult).then_inc(wln, 1)
            for m in range(ET):
                rope_h, rope_l = (a[:, m, KC:VC].rearrange("p (h c) -> p h c", h=H)[:, :, 0:RD] for a in (wh, wl))
                src = w_cols_raw[:, m, 0:H * RD].rearrange("p (h c) -> p h c", h=H)
                copy(rope_h, src).then_inc(wfh, 1)
                dve.wait_ge(wfh, 2 * m + 1)
                minus(rope_l, src, rope_h).then_inc(wdone, 1)
                dve.wait_ge(wln, m + 1)
                src = w_cols_raw[:, m, H * RD:]
                copy(wh[:, m, Q2C:WC], src).then_inc(wfh, 1)
                dve.wait_ge(wfh, 2 * m + 2)
                minus(wl[:, m, Q2C:WC], src, wh[:, m, Q2C:WC]).then_inc(wdone, 1)

            def copy_batch(b):
                dve.wait_ge(tr0, b)
                dve.wait_ge(v2d, 2 * b)
                copy(xb[:, :, :], xn[:, bass.ds(2 * b, 2), :])
                copy(rb[:, :], rms1[:, bass.ds(2 * b, 2)]).then_inc(xbd, 1)

            def stage_xt(b):
                dve.wait_ge(xthd, b + 1)
                minus(xtl[:, :, :].rearrange("p e t -> p (e t)"), ps[2][:, :],
                      xth[:, :, :].rearrange("p e t -> p (e t)")).then_inc(xtld, 1)

            def stage_p1(b):
                for n in range(16):
                    tt = n // 8
                    i = 9 * tt + n % 8
                    dve.wait_ge(p1d, 18 * b + i + 1)
                    dve.wait_ge(tr1, 16 * b + max(n - 3, 0))
                    dve.wait_ge(tokd, 16 * b + max(n - 1, 0))
                    a = ps[i % 2][:, 0:CH].rearrange("p (h c) -> p h c", h=G)
                    nc.vector.tensor_tensor(tok[:, n % 4, :, 0:HW], a,
                                            cos_t[:, tt:tt + 1, :].broadcast_to([P, G, HW]), ALU.mult)
                    sw = a[:, :, 0:RD].rearrange("p h (s d) -> p h s d", s=2)[:, :, ::-1, :]
                    sn = sin_t[:, tt:tt + 1, :].broadcast_to([P, G, RD]).rearrange("p h (s d) -> p h s d", s=2)
                    nc.vector.tensor_tensor(swp[:, n % 2, :, :].rearrange("p h (s d) -> p h s d", s=2), sw, sn,
                                            ALU.mult).then_inc(roped, 1)

            def stage_m1(b):
                dve.wait_ge(qke, 16 * b + 16)
                dve.wait_ge(mtr1, b)

                def rounded(g):
                    dve.wait_ge(m1d, 16 * b + 2 * max(g - 1, 0))
                    copy(qr[:, g % 2, :, :], qt[:, 2 * g:2 * g + 2, :])
                    copy(kr[:, g % 2, :, :], kt[:, 2 * g:2 * g + 2, :]).then_inc(rrd, 1)

                rounded(0)
                for h in range(H):
                    if h % 2 == 0 and h + 2 < H:
                        rounded(h // 2 + 1)
                    maxima(b, h, h, negm1, m1d, mx1)

            def maxima(b, h, col, negm, md, mx):
                dve.wait_ge(md, 16 * b + h + 1)
                o = ps[4 + h % 2]
                nc.vector.tensor_reduce(negm[:, 0, col:col + 1], o[:, 0:P], AX.X, ALU.max, negate=True)
                nc.vector.tensor_reduce(negm[:, 1, col:col + 1], o[:, S:2 * S], AX.X, ALU.max,
                                        negate=True).then_inc(mx, 1)

            def stage_p2(b):
                for tt in range(2):
                    dve.wait_ge(y2d, 2 * b + tt + 1)
                    dve.wait_ge(tr2, 8 * b + 4 * tt)
                    q, k = y2[:, 0, :, :], y2[:, 1, :, :]
                    copy(qs[:, :, 0:D], q)
                    copy(qs[:, :, D:2 * D], q)
                    copy(ks[:, :, 0:D], k)
                    copy(ks[:, :, 2 * D:3 * D], k).then_inc(hi2, 1)
                    dve.wait_ge(hi2, 2 * b + tt + 1)
                    minus(qs[:, :, 2 * D:3 * D], q, qs[:, :, 0:D])
                    minus(ks[:, :, D:2 * D], k, ks[:, :, 0:D]).then_inc(s2d, 1)

            def stage_t(b, pv, rc, ot_, before):
                before()
                for g in range(NG):
                    dve.wait_ge(pv, NG * b + g + 1)
                    if g:
                        dve.wait_ge(ot_, NG * b + g)
                    nc.vector.reciprocal(rec[:, :], ps[7][:, 0:S]).then_inc(rc, 1)
                    dve.wait_ge(rc, NG * b + g + 1)
                    nc.vector.tensor_tensor(ot[:, g, :], ps[6][:, 0:S], rec[:, :], ALU.mult).then_inc(ot_, 1)

            def batch(b, more):
                stage_m1(b)
                stage_p2(b)
                stage_t(b, pv1, rc1, ot1, lambda: (dve.wait_ge(o2, 2 * b), dve.wait_ge(ot2, NG * b)))
                for tt in range(2):
                    dve.wait_ge(o1, 2 * b + tt + 1)
                    copy(s_tok[:, bass.ds(2 * b + tt, 1), :].rearrange("p o e -> p (o e)"),
                         ps[tt][:, 0:E]).then_inc(sd, 1)
                if more:
                    copy_batch(b + 1)
                dve.wait_ge(mtr2, b)
                for h in range(H):
                    maxima(b, h, (h % 2) * (H // 2) + h // 2, negm2, m2d, mx2)
                if more:
                    stage_xt(b + 1)
                    stage_p1(b + 1)
                stage_t(b, pv2, rc2, ot2, lambda: (dve.wait_ge(o1, 2 * b + 2), dve.wait_ge(ot1, NG * b + NG)))
                for tt in range(2):
                    dve.wait_ge(o2, 2 * b + tt + 1)
                    a = xn[:, bass.ds(2 * b + tt, 1), :].rearrange("p o e -> p (o e)")
                    nc.vector.tensor_tensor(a, ps[tt][:, 0:E], a, ALU.add).then_inc(x2d, 1)

            dve.wait_ge(rmd, 1)
            copy_batch(0)
            stage_xt(0)
            stage_p1(0)
            with dve.Fori(0, last) as b:
                batch(b, True)
            batch(last, False)

            dve.wait_ge(x2d, TT)
            norm_stats(st_a, st_c, 2 * TT)
            dve.wait_ge(st_c, TT)
            nc.vector.tensor_tensor(msq[:, :], mv[:, :, 0], mv[:, :, 0], ALU.mult).then_inc(ms2, 1)
            dve.wait_ge(ms2, 1)
            nc.vector.scalar_tensor_tensor(out=msq[:, :], in0=msq[:, :], scalar=EPS, in1=mv[:, :, 1],
                                           op0=ALU.add, op1=ALU.add).then_inc(ms2, 1)
            dve.wait_ge(rm2, 1)
            with dve.Fori(0, TT // 2) as i:
                for s in range(2):
                    dve.wait_ge(tr3, 2 * i)
                    nc.vector.tensor_scalar(xb2[:, s, :], xn[:, bass.ds(2 * i + s, 1), :].rearrange("p o e -> p (o e)"),
                                            rstd[:, bass.ds(2 * i + s, 1)], None, ALU.mult).then_inc(xb2d, 1)
                for s in range(2):
                    dve.wait_ge(ytd, 2 * i + s + 1)
                    t = bass.ds((2 * i + s) * P, P)
                    copy(x2h[:, :, t], yt[:, s, :, :]).then_inc(x2hd, 1)
                    dve.wait_ge(x2hd, 2 * i + s + 1)
                    minus(x2l[:, :, t], yt[:, s, :, :], x2h[:, :, t]).then_inc(x2ld, 1)
                    dve.wait_ge(lgd, 2 * i + s + 1)
                    copy(lg[:, bass.ds(2 * i + s, 1), :].rearrange("p o n -> p (o n)"), ps[2 + s][:, 0:NE]).then_inc(lgk, 1)

            for t in range(TT):
                dve.wait_ge(lgk, t + 1)
                nc.vector.max(mx[:, t, :], lg[:, t, :]).then_inc(top, 1)
                dve.wait_ge(top, 2 * t + 1)
                nc.vector.max_index(ix[:, t, :], mx[:, t, :], lg[:, t, :]).then_inc(top, 1)
            dve.wait_ge(top, 2 * TT)
            nc.vector.tensor_tensor(gate[:, 0, :], mx[:, :, 1], mx[:, :, 0], ALU.subtract).then_inc(gch, 1)
            copy(ixf[:, :, :], ix[:, :, 0:2])
            dve.wait_ge(gex, 1)
            nc.vector.tensor_scalar(gate[:, 0, :], gate[:, 1, :], 1.0, None, ALU.add).then_inc(gch, 1)
            dve.wait_ge(gch, 2)
            nc.vector.reciprocal(gate[:, 2, :], gate[:, 0, :]).then_inc(gch, 1)
            dve.wait_ge(gch, 3)
            nc.vector.tensor_tensor(gate[:, 3, :], gate[:, 1, :], gate[:, 2, :], ALU.mult).then_inc(gch, 1)
            dve.wait_ge(gch, 4)
            dve.wait_ge(xrd, 32)
            for j in range(2):
                nc.vector.tensor_tensor(pick[:, j, :, :], iot[:, :, :],
                                        ixf[:, :, j:j + 1].broadcast_to([P, TT, NE]), ALU.is_equal).then_inc(gch, 1)
                dve.wait_ge(gch, 5 + 2 * j)
                nc.vector.tensor_tensor(pick[:, j, :, :], pick[:, j, :, :],
                                        gate[:, 2 + j, :].unsqueeze(2).broadcast_to([P, TT, NE]),
                                        ALU.mult).then_inc(gch, 1)
                dve.wait_ge(gch, 6 + 2 * j)
            nc.vector.tensor_tensor(cw[:, :, :].rearrange("p n t -> p t n"), pick[:, 0, :, :], pick[:, 1, :, :],
                                    ALU.add).then_inc(cwd, 1)
            dve.wait_ge(cwd, 1)

            def split_expert(e, s):
                dve.wait_ge(rawd[s], 8 * e + 16 - 8 * s)
                dve.wait_ge(dd, 16 * e - 16 if not isinstance(e, int) or e else 0)
                copy(weh[:, s, :], raw[:, s, :]).then_inc(wehd, 1)
                dve.wait_ge(wehd, e + 1)
                minus(wel[:, s, :], raw[:, s, :], weh[:, s, :]).then_inc(weld, 1)

            def product(n, it):
                dve.wait_ge(ud, n + 1)
                dve.wait_ge(sgd, n + 1)
                nc.vector.tensor_tensor(hf[:, it % 2, :], ps[2 + it % 2][:, :], sg[:, it % 2, :],
                                        ALU.mult).then_inc(hfd, 1)
                dve.wait_ge(hfd, n + 1)
                copy(hh[:, it % 2, :], hf[:, it % 2, :]).then_inc(hhd, 1)
                dve.wait_ge(hhd, n + 1)
                minus(hl[:, it % 2, :], hf[:, it % 2, :], hh[:, it % 2, :]).then_inc(hld, 1)

            def add_y(e, c):
                dve.wait_ge(dd, 16 * e + 4 * c + 4)
                for t in range(TC // P):
                    a = xn[:, bass.ds(4 * c + t, 1), :].rearrange("p o e -> p (o e)")
                    w_ = cw[:, bass.ds(e, 1), bass.ds(4 * c + t, 1)].rearrange("p a b -> p (a b)")
                    i = nc.vector.scalar_tensor_tensor(out=a, in0=ps[4 + t // 2][:, (t % 2) * E:(t % 2 + 1) * E],
                                                       scalar=w_, in1=a, op0=ALU.mult, op1=ALU.add)
                i.then_inc(yd, 1)

            def expert(e, s, final):
                def chunk(c, n):
                    for it in range(1, IT):
                        product(n + it, it)
                    if not (final and isinstance(c, int)):
                        product(n + IT, 0)
                    add_y(e, c)
                if not final:
                    chunk(0, 16 * e)
                    split_expert(e + 1, 1 - s)
                    with dve.Fori(1, NC) as c:
                        chunk(c, 16 * e + 4 * c)
                else:
                    with dve.Fori(0, NC - 1) as c:
                        chunk(c, 16 * e + 4 * c)
                    chunk(NC - 1, 16 * e + 4 * (NC - 1))

            def split_first():
                dve.wait_ge(rawd[0], 16)
                copy(weh[:, 0, :], raw[:, 0, :]).then_inc(wehd, 1)
                dve.wait_ge(wehd, 1)
                minus(wel[:, 0, :], raw[:, 0, :], weh[:, 0, :]).then_inc(weld, 1)

            split_first()
            product(0, 0)
            with dve.Fori(0, NE // 2 - 1) as i:
                for s in range(2):
                    expert(2 * i + s, s, False)
            expert(NE - 2, 0, False)
            expert(NE - 1, 1, True)

            for j in range(TT // 4):
                t = slice(4 * j, 4 * j + 4)
                dve.wait_ge(gld, j + 1)
                nc.vector.tensor_tensor(s_tok[:, t, :], s_tok[:, t, :], gl[:, :, :], ALU.mult).then_inc(mud, 1)
                dve.wait_ge(mud, j + 1)
                nc.vector.tensor_tensor(xr[:, t, :], xr[:, t, :], s_tok[:, t, :], ALU.add).then_inc(fin, 1)


def laid_out(f):
    a = {k: np.asarray(v) for k, v in f.items()}
    dt = np.float32

    def per_head(w, rows):
        return w.reshape(H, rows, w.shape[1])

    def padded(w):
        o = np.zeros((H, PADV, E), dt)
        o[:, :D, :] = w.T.reshape(H, D, E)
        return o.reshape(H * PADV, E)

    w_uqr = np.concatenate([per_head(a["L0_attn_w_qr"], RD), per_head(a["L0_attn_w_uq"], D)], 1).reshape(H * HW, CQ).T
    w_ukv = np.concatenate([a["L0_attn_w_uk"], a["L0_attn_w_uv"]], 0).T
    w_cols = np.concatenate([a["L0_attn_w_kr"], a["L0_ffn_Wq"], a["L0_ffn_Wk"], a["L0_ffn_Wv"]], 0).T

    def lhs(w):
        return w.T.reshape(ET, P, FF).transpose(1, 0, 2).reshape(P, ET * FF)

    experts = np.stack([np.concatenate([
        lhs(a["L0_ffn_Wg"][e]), lhs(a["L0_ffn_Wu"][e]),
        a["L0_ffn_Wd"][e].T.reshape(IT, P, E).transpose(1, 0, 2).reshape(P, IT * E)], 1) for e in range(NE)])

    pos = np.arange(S, dtype=dt)
    inv = (1.0 / 10000.0 ** (np.arange(0, RD, 2, dtype=dt) / RD)).astype(dt)
    ang = (pos[:, None] * inv[None, :]).astype(dt)
    c, s = np.cos(ang), np.sin(ang)
    cosines = np.concatenate([c, c, np.ones((S, D), dt)], 1).reshape(2, P, HW).transpose(1, 0, 2)
    sines = np.concatenate([-s, s], 1).reshape(2, P, RD).transpose(1, 0, 2)
    i = np.arange(P)
    mask = np.where(i[None, :] > i[:, None], BIG, 0.0)
    consts = dict(cosines=cosines, sines=sines, ident=np.eye(P), mask=mask, mask_t=mask.T,
                  experts_iota=np.broadcast_to(np.arange(NE), (P, TT, NE)))
    r = dict(
        x=a["L0_attn_x"].reshape(T, E), w_cols=w_cols, w_dq=a["L0_attn_w_dq"], w_uqr=w_uqr,
        w_dkv=a["L0_attn_w_dkv"], w_ukv=w_ukv, w_out=padded(a["L0_attn_w_out"]), w_o=padded(a["L0_ffn_Wo"]),
        w_ln1=a["L0_ffn_w_ln1"].reshape(ET, P).T, w_ln2=a["L0_ffn_w_ln2"].reshape(ET, P).T,
        w_r=a["L0_ffn_Wr"].T, w_experts=experts, **{k: v.astype(dt) for k, v in consts.items()})
    return {k: np.ascontiguousarray(v) for k, v in r.items()}


def kernel(**inputs):
    import concourse.bacc as bacc
    from concourse.bass_utils import run_bass_kernel_spmd

    nc = bacc.Bacc("TRN2", target_bir_lowering=False, num_devices=1)
    arrays = laid_out(inputs)
    args = {k: nc.dram_tensor(f"in_{k}", v.shape, mybir.dt.from_np(v.dtype), kind="ExternalInput").ap()
            for k, v in arrays.items()}
    out = nc.dram_tensor("out_0", (T, E), F32, kind="ExternalOutput").ap()
    build(nc, out=out, **args)
    r = run_bass_kernel_spmd(nc, [{f"in_{k}": v for k, v in arrays.items()}], core_ids=[0])
    return r.results[0]["out_0"].reshape(B, S, E)
```

```python
from contextlib import ExitStack

import numpy as np

import concourse.bass as bass
from concourse import mybir

F32 = mybir.dt.float32
F32R = mybir.dt.float32r
BF16 = mybir.dt.bfloat16
U32 = mybir.dt.uint32
ALU = mybir.AluOpType
ACT = mybir.ActivationFunctionType
AX = mybir.AxisListType

P = 128
B, S, E = 8, 256, 256
H, D, RD = 16, 16, 64
CQ, CKV = 192, 64
NE, FF = 8, 512
T = B * S
TT = T // P
ET = E // P
HW = RD + D
MROW = HW
G = 4
NG = H // G
PADV = 32
ST = 64
MROW2 = 3 * D
V1 = D
QC, KC, VC = 0, H * HW, 2 * H * HW
Q2C = VC + H * D
V2C = Q2C + 2 * H * D
WC = V2C + H * D
CH = G * HW
EPS = 1e-5
BIG = -1e30
IT = FF // P
TC = 512
NC = T // TC
WG, WU, WD = 0, ET * FF, 2 * ET * FF
WE = WD + IT * E


def wait(engine, semaphore, value):
    if not isinstance(value, int) or value > 0:
        engine.wait_ge(semaphore, value)


def build(nc, x, w_cols, w_dq, w_uqr, w_dkv, w_ukv, w_out, w_o, w_ln1, w_ln2, w_r, w_experts,
          cosines, sines, ident, mask, mask_t, experts_iota, out):
    ctx = ExitStack()
    with ctx:
        def sb(name, shape, dt=F32, stack=ctx):
            return stack.enter_context(nc.sbuf_tensor(name, shape, dt))

        def sem(name):
            return ctx.enter_context(nc.semaphore(name))

        xn = sb("xn", [P, TT, E])
        s_dram = nc.dram_tensor("mla_branch", (T, E), F32).ap()
        s_view = s_dram.rearrange("(t p) e -> p t e", p=P)
        idf = sb("idf", [P, P])
        ln2 = sb("ln2", [P, ET])
        wr = sb("wr", [P, ET, NE])
        rms1 = sb("rms1", [P, TT])
        mv = sb("mv", [P, TT, 2])
        stats = sb("stats", [P, TT, 6])
        msq = sb("msq", [P, TT])
        rstd = sb("rstd", [P, TT])
        mhalf = sb("mhalf", [P, TT])

        att = ExitStack()
        cos_t = sb("cos_t", [P, ET, HW], F32, att)
        sin_t = sb("sin_t", [P, ET, RD], F32, att)
        idb = sb("idb", [P, P], BF16, att)
        maskb = sb("maskb", [P, 2, P], BF16, att)
        wh = sb("wh", [P, ET, WC], F32R, att)
        wl = sb("wl", [P, ET, WC], F32R, att)
        wo1 = sb("wo1", [P, ET, E], F32, att)
        wo2 = sb("wo2", [P, ET, E], F32, att)
        ln1 = sb("ln1", [P, ET], F32, att)
        xb = sb("xb", [P, 2, E], F32, att)
        rb = sb("rb", [P, 2], F32, att)
        xth = sb("xth", [P, ET, S], F32R, att)
        xtl = sb("xtl", [P, ET, S], F32R, att)
        tok = sb("tok", [P, 4, G, P], F32, att)
        swp = sb("swp", [P, 2, G, RD], F32, att)
        qr = sb("qr", [P, 2, 2, S], F32R, att)
        kr = sb("kr", [P, 2, 2, S], F32R, att)
        y2 = sb("y2", [P, 2, H, D], F32, att)
        qs = sb("qs", [P, H, ST], F32R, att)
        ks = sb("ks", [P, H, ST], F32R, att)
        qt2 = sb("qt2", [P, H, S], F32R, att)
        kt2 = sb("kt2", [P, H // 2, S], F32R, att)
        v1 = sb("v1", [P, 2, H, PADV], F32, att)
        v2 = sb("v2", [P, 2, H, PADV], F32, att)
        ex = sb("ex", [P, 2 * G, 3 * P], F32, att)
        ov = sb("ov", [P, NG, S], F32, att)
        rec = sb("rec", [P, 2, H], F32, att)
        otk = sb("otk", [P, 2, H, D], F32, att)
        otf = sb("otf", [P, ET, S], F32, att)
        s_b = sb("s_b", [P, 2, E], F32, att)
        negm1 = sb("negm1", [P, 2, H], F32, att)
        negm2 = sb("negm2", [P, 2, H], F32, att)
        mt1 = sb("mt1", [H, S], F32, att)
        mt2 = sb("mt2", [H, S], F32R, att)
        prep = ExitStack()
        mask_f = sb("mask_f", [P, 2, P], F32, prep)
        w_cols_raw = sb("w_cols_raw", [P, ET, H * RD + 3 * E], F32, prep)
        w_uqr_raw = sb("w_uqr_raw", [P, 2, H * HW], F32, prep)
        w_dq_raw = sb("w_dq_raw", [P, 2, E], F32, prep)
        w_dkv_raw = sb("w_dkv_raw", [CKV, E], F32, prep)
        w_ukv_raw = sb("w_ukv_raw", [CKV, 2 * H * D], F32, prep)
        prep.close()
        qt = sb("qt", [P, H, S], F32, att)
        kt = sb("kt", [P, H, S], F32, att)
        att.close()

        moe = ExitStack()
        raw = sb("raw", [P, 2, WE], F32, moe)
        weh = sb("weh", [P, 2, WE], F32R, moe)
        wel = sb("wel", [P, 2, WE], F32R, moe)
        x2h = sb("x2h", [P, ET, T], F32R, moe)
        x2l = sb("x2l", [P, ET, T], F32R, moe)
        xb2 = sb("xb2", [P, 4, E], F32, moe)
        yt = sb("yt", [P, 4, ET, P], F32, moe)
        lg = sb("lg", [P, TT, NE], F32, moe)
        mx = sb("mx", [P, TT, NE], F32, moe)
        ix = sb("ix", [P, TT, NE], U32, moe)
        ixf = sb("ixf", [P, TT, 2], F32, moe)
        iot = sb("iot", [P, TT, NE], F32, moe)
        gate = sb("gate", [P, 4, TT], F32, moe)
        pick = sb("pick", [P, 2, TT, NE], F32, moe)
        cw = sb("cw", [P, NE, TT], F32, moe)
        sg = sb("sg", [P, 2, TC], F32, moe)
        hf = sb("hf", [P, 2, TC], F32, moe)
        hh = sb("hh", [P, 2, TC], F32R, moe)
        hl = sb("hl", [P, 2, TC], F32R, moe)
        xr = sb("xr", [P, TT, E], F32, moe)
        s_tok = sb("s_tok", [P, TT, E], F32, moe)
        gl = sb("gl", [P, 4, E], F32, moe)
        moe.close()

        ps = [ctx.enter_context(nc.psum_tensor(f"ps{i}", [P, 512], F32)) for i in range(8)]

        s_lr = sem("low_rank_weights_loaded")
        s_w = sem("direct_weights_loaded")
        s_c = sem("late_weights_loaded")
        s_k = sem("constants_loaded")
        s_x = [sem("x_first_half_loaded"), sem("x_second_half_loaded")]
        cast = sem("masks_cast")
        clear = sem("pads_set")
        comb = sem("weights_combined")
        combh = sem("combined_high")
        combl = sem("combined_low")
        wfh = sem("direct_high")
        wdone = sem("direct_low")
        st_a = sem("stats_taken")
        st_b = sem("stats_joined")
        powd = sem("rstd_ready")
        xnd = sem("xn_ready")
        msd = sem("mean_squares")
        rmd = sem("rms1_ready")
        xbd = sem("batch_copied")
        rbd = sem("rms1_copied")
        tr0 = sem("xT_transposed")
        xthd = sem("xT_high")
        xtld = sem("xT_low")
        p1d = sem("mla_projected")
        roped = sem("rope_products")
        tokd = sem("rope_done")
        tr1 = sem("mla_transposed")
        qke = sem("mla_qk_kept")
        v1d = sem("mla_v_kept")
        rrd = sem("mla_qk_rounded")
        m1d = sem("mla_scores")
        mx1 = sem("mla_max")
        mtr1 = sem("mla_max_transposed")
        mte1 = sem("mla_max_kept")
        md1 = sem("mla_max_row")
        st1 = sem("mla_scores_t")
        ex1 = sem("mla_exp")
        pv1 = sem("mla_pv")
        ov1 = sem("mla_heads_kept")
        fa1 = sem("mla_heads_to_tokens")
        rc1 = sem("mla_reciprocal")
        on1 = sem("mla_heads_normalised")
        fb1 = sem("mla_heads_back")
        of1 = sem("mla_heads_back_kept")
        o1 = sem("mla_out")
        sd = sem("mla_out_kept")
        sst = sem("mla_out_stored")
        p2d = sem("mha_projected")
        y2d = sem("mha_qk_scaled")
        v2d = sem("mha_v_kept")
        hi2 = sem("mha_qk_high")
        s2d = sem("mha_qk_stacked")
        tr2 = sem("mha_transposed")
        t2e = sem("mha_qk_kept")
        m2d = sem("mha_scores")
        mx2 = sem("mha_max")
        mtr2 = sem("mha_max_transposed")
        mte2 = sem("mha_max_kept")
        md2 = sem("mha_max_row")
        st2 = sem("mha_scores_t")
        ex2 = sem("mha_exp")
        pv2 = sem("mha_pv")
        ov2 = sem("mha_heads_kept")
        fa2 = sem("mha_heads_to_tokens")
        rc2 = sem("mha_reciprocal")
        on2 = sem("mha_heads_normalised")
        fb2 = sem("mha_heads_back")
        of2 = sem("mha_heads_back_kept")
        o2 = sem("mha_out")
        x2d = sem("ffn_residual")
        st_c = sem("stats2_taken")
        st_d = sem("stats2_joined")
        ms2 = sem("mean_squares2")
        rm2 = sem("rms2_ready")
        xb2d = sem("x2_scaled")
        tr3 = sem("x2_transposed")
        ytd = sem("x2T_scaled")
        x2hd = sem("x2T_high")
        x2ld = sem("x2T_low")
        lgd = sem("router_logits")
        lgk = sem("logits_kept")
        top = sem("top2_found")
        gch = sem("gate_steps")
        gex = sem("gate_exp")
        cwd = sem("expert_weights_ready")
        rawd = [sem("expert_loaded_even"), sem("expert_loaded_odd")]
        wehd = sem("expert_high")
        weld = sem("expert_low")
        gd = sem("hg_done")
        ud = sem("hu_done")
        sgd = sem("silu_done")
        hfd = sem("h_done")
        hhd = sem("h_high")
        hld = sem("h_low")
        dd = sem("down_done")
        yd = sem("y_added")
        xrd = sem("x_again")
        gld = sem("ffn_silu")
        mud = sem("branches_multiplied")
        fin = sem("result_ready")
        s_out = sem("stored")

        last = B - 1
        N_DIRECT = 2 * ET
        N_COMB = ET * (NG + 1)

        def rope_part(w, m):
            return w[:, m, KC:VC].rearrange("p (h c) -> p h c", h=H)[:, :, 0:RD]

        block = ctx.enter_context(nc.Block())

        @block.sync
        def _(sp):
            for dst, src in ((w_dq_raw[0:P, 0, :], w_dq[0:P, :]), (w_dq_raw[0:CQ - P, 1, :], w_dq[P:CQ, :]),
                             (w_uqr_raw[0:P, 0, :], w_uqr[0:P, :]), (w_uqr_raw[0:CQ - P, 1, :], w_uqr[P:CQ, :]),
                             (w_dkv_raw[:, :], w_dkv), (w_ukv_raw[:, :], w_ukv)):
                sp.dma_start(dst, src).then_inc(s_lr, 16)
            for dst, src in ((w_cols_raw[:, :, :], w_cols.rearrange("(m p) n -> p m n", p=P)),
                             (ln1[:, :], w_ln1)):
                sp.dma_start(dst, src).then_inc(s_w, 16)
            for dst, src in ((ln2[:, :], w_ln2),
                             (wr[:, :, :], w_r.rearrange("(m p) n -> p m n", p=P)),
                             (wo1[:, :, :], w_out.rearrange("(m p) e -> p m e", p=P)),
                             (wo2[:, :, :], w_o.rearrange("(m p) e -> p m e", p=P))):
                sp.dma_start(dst, src).then_inc(s_c, 16)

            def row1(b):
                sp.wait_ge(mte1, b + 1)
                sp.dma_start(qt[MROW:MROW + 1, :, :], mt1[:, :]).then_inc(md1, 16)

            with sp.Fori(0, B) as b:
                row1(b)
                sp.wait_ge(mte2, b + 1)
                for e in range(2):
                    r = ST * e + MROW2
                    sp.dma_start(qt2[r:r + 1, e:H:2, :].bitcast(F32),
                                 mt2[e * H // 2:(e + 1) * H // 2, :].bitcast(F32)).then_inc(md2, 16)
                sp.wait_ge(sd, b + 1)
                sp.dma_start(s_view[:, bass.ds(2 * b, 2), :], s_b[:, :, :]).then_inc(sst, 16)

            sp.wait_ge(x2d, B)
            sp.wait_ge(sst, 16 * B)

            def load(e, s):
                sp.dma_start(raw[:, s, :], w_experts[e, :, :]).then_inc(rawd[s], 16)
            load(0, 0)
            load(1, 1)
            sp.dma_start(iot[:, :, :], experts_iota).then_inc(xrd, 16)
            sp.dma_start(xr[:, :, :], x.rearrange("(t p) e -> p t e", p=P)).then_inc(xrd, 16)
            sp.dma_start(s_tok[:, :, :], s_view).then_inc(xrd, 16)
            with sp.Fori(0, NE // 2 - 1) as i:
                for s in range(2):
                    sp.wait_ge(weld, 2 * i + s + 1)
                    sp.dma_start(raw[:, s, :],
                                 w_experts[bass.ds(2 * i + s + 2, 1), :, :].rearrange("o p n -> (o p) n")
                                 ).then_inc(rawd[s], 16)
            o_v = out.rearrange("(t p) e -> p t e", p=P)
            for j in range(TT // 4):
                sp.wait_ge(fin, j + 1)
                sp.dma_start(o_v[:, 4 * j:4 * j + 4, :], xr[:, 4 * j:4 * j + 4, :]).then_inc(s_out, 16)
            sp.wait_ge(s_out, 16 * (TT // 4))

        @block.gpsimd
        def _(pool):
            nc.gpsimd.memset(mhalf[:, :], -0.5)
            nc.gpsimd.memset(tok[:, :, :, RD:P], 0.0)
            nc.gpsimd.memset(v1[:, :, :, :], 0.0)
            nc.gpsimd.memset(v2[:, :, :, :], 0.0)
            nc.gpsimd.memset(ks[:, :, :].bitcast(F32), 0.0)
            nc.gpsimd.memset(qs[:, :, :].bitcast(F32), 0.0).then_inc(clear, 1)
            pool.wait_ge(clear, 1)
            nc.gpsimd.memset(v1[:, :, :, V1:V1 + 1], 1.0)
            nc.gpsimd.memset(v2[:, :, :, V1:V1 + 1], 1.0)
            nc.gpsimd.memset(tok[:, 1:4:2, :, MROW:MROW + 1], 1.0)
            nc.gpsimd.memset(ks[:, :, MROW2:MROW2 + 1].bitcast(F32), 1.0)
            nc.gpsimd.memset(qt2[:, :, :].bitcast(F32), 0.0).then_inc(clear, 1)

            pool.wait_ge(st_b, TT + 1)
            nc.gpsimd.tensor_tensor(rstd[:, :], msq[:, :], mhalf[:, :], ALU.pow).then_inc(powd, 1)
            pool.wait_ge(msd, 3)
            nc.gpsimd.tensor_tensor(rms1[:, :], msq[:, :], mhalf[:, :], ALU.pow).then_inc(rmd, 1)

            with pool.Fori(0, B) as b:
                for n in range(2 * 2 * NG):
                    pool.wait_ge(roped, 16 * b + n + 1)
                    t = tok[:, n % 4, :, 0:RD]
                    nc.gpsimd.tensor_tensor(t, t, swp[:, n % 2, :, :], ALU.add).then_inc(tokd, 1)

            pool.wait_ge(ms2, 2)
            nc.gpsimd.tensor_tensor(rstd[:, :], msq[:, :], mhalf[:, :], ALU.pow).then_inc(rm2, 1)

        def order(step_proj, step_tr, after):
            for i in range(2 * 9 + 2):
                if i < 18:
                    step_proj(i)
                if i >= 2 and (i - 2) % 9 != 8:
                    step_tr(i - 2, 8 * ((i - 2) // 9) + (i - 2) % 9)
                after.get(i, lambda: None)()

        @block.tensor
        def _(pe):
            def mm(o, a, m, start, stop, **k):
                return nc.tensor.matmul(o, a, m, start=start, stop=stop, skip_group_check=True, **k)

            pe.wait_ge(s_lr, 16 * 6)
            w = 0
            for m in range(ET):
                cols = slice(m * P, (m + 1) * P)
                for c in range(NG + 1):
                    if w >= 8:
                        pe.wait_ge(combl, w - 7)
                    if c < NG:
                        o = ps[w % 8][:, 0:CH]
                        mm(o, w_dq_raw[:, 0, cols], w_uqr_raw[:, 0, c * CH:(c + 1) * CH], True, False)
                        i = mm(o, w_dq_raw[0:CQ - P, 1, cols], w_uqr_raw[0:CQ - P, 1, c * CH:(c + 1) * CH],
                               False, True)
                    else:
                        i = mm(ps[w % 8][:, :], w_dkv_raw[:, cols], w_ukv_raw[:, :], True, True)
                    i.then_inc(comb, 1)
                    w += 1

            def proj(o, c0, n, tt):
                t = slice(tt * P, (tt + 1) * P)
                k = 0
                for a, m in ((xth, wh), (xth, wl), (xtl, wh)):
                    for e in range(ET):
                        i = mm(o, a[:, e, t], m[:, e, c0:c0 + n], k == 0, k == 2 * 3 - 1)
                        k += 1
                return i

            def max_t(b, negm, mx, mtr):
                wait(pe, mx, 16 * b + H)
                for t in range(2):
                    i = nc.tensor.transpose(ps[2][0:H, t * P:(t + 1) * P], negm[:, t, :], idf[:, :])
                i.then_inc(mtr, 1)

            def project_heads(b, ov_, fa, on_, fb, of_, wo, od):
                def to_tokens():
                    wait(pe, ov_, NG * b + NG)
                    for tt in range(2):
                        for g in range(NG):
                            i = nc.tensor.transpose(ps[6 + tt][:, g * P:(g + 1) * P],
                                                    ov[:, g, tt * P:(tt + 1) * P], idf[:, :])
                    i.then_inc(fa, 1)

                def back():
                    wait(pe, on_, b + 1)
                    for e in range(ET):
                        for tt in range(2):
                            a = otk[:, tt, :, :].rearrange("p h c -> p (h c)")[:, e * P:(e + 1) * P]
                            i = nc.tensor.transpose(ps[6][:, (2 * e + tt) * P:(2 * e + tt + 1) * P], a, idf[:, :])
                    i.then_inc(fb, 1)

                def project():
                    wait(pe, of_, b + 1)
                    for tt in range(2):
                        for e in range(ET):
                            i = mm(ps[7][:, tt * E:(tt + 1) * E], otf[:, e, tt * P:(tt + 1) * P], wo[:, e, :],
                                   e == 0, e == ET - 1)
                    i.then_inc(od, 1)
                return to_tokens, back, project

            def close1(b):
                return project_heads(b, ov1, fa1, on1, fb1, of1, wo1, o1)

            def close2(b):
                return project_heads(b, ov2, fa2, on2, fb2, of2, wo2, o2)

            def stage_p1(b, after):
                wait(pe, mx2, 16 * b)
                wait(pe, xbd, b + 1)
                for e in range(ET):
                    for tt in range(2):
                        i = nc.tensor.transpose(ps[3][:, (2 * e + tt) * P:(2 * e + tt + 1) * P],
                                                xb[:, tt, e * P:(e + 1) * P], idf[:, :])
                i.then_inc(tr0, 1)
                if not isinstance(b, int) or b > 0:
                    max_t(b - 1, negm2, mx2, mtr2)
                wait(pe, y2d, 2 * b)
                wait(pe, v2d, 2 * b)
                wait(pe, xtld, b + 1)

                def step_proj(i):
                    tt, c = i // 9, i % 9
                    if i >= 2:
                        j = i - 2
                        if j % 9 == 8:
                            wait(pe, v1d, 2 * b + j // 9 + 1)
                        else:
                            wait(pe, roped, 16 * b + 8 * (j // 9) + j % 9 + 1)
                    if c < 8:
                        c0 = (QC, KC)[c % 2] + (c // 2) * CH
                        proj(ps[i % 2][:, 0:CH], c0, CH, tt).then_inc(p1d, 1)
                    else:
                        proj(ps[i % 2][:, 0:H * D], VC, H * D, tt).then_inc(p1d, 1)

                def step_tr(i, n):
                    wait(pe, tokd, 16 * b + n + 1)
                    if n == 0:
                        wait(pe, mte2, b)
                    if n >= 2:
                        wait(pe, qke, 16 * b + n - 1)
                    for j in range(G):
                        t = nc.tensor.transpose(ps[2 + n % 2][:, j * P:(j + 1) * P], tok[:, n % 4, j, :],
                                                idf[:, :])
                    t.then_inc(tr1, 1)

                order(step_proj, step_tr, after)

            def stage_p2(b, after):
                max_t(b, negm1, mx1, mtr1)
                wait(pe, roped, 16 * b + 16)
                wait(pe, v1d, 2 * b + 2)
                for j in range(4):
                    tt = j // 2
                    if j >= 2:
                        wait(pe, (y2d, v2d)[j % 2], 2 * b + 1)
                    if j % 2 == 0:
                        proj(ps[0][:, :], Q2C, 2 * H * D, tt).then_inc(p2d, 1)
                    else:
                        proj(ps[1][:, 0:H * D], V2C, H * D, tt).then_inc(p2d, 1)
                    after.get(j, lambda: None)()
                wait(pe, mte1, b + 1)
                for u in range(8):
                    if u % 4 == 0:
                        wait(pe, s2d, 2 * b + u // 4 + 1)
                    if u >= 2:
                        wait(pe, t2e, 8 * b + u - 1)
                    a = (qs, ks)[u % 4 // 2][:, :, :].rearrange("p h c -> p (h c)").bitcast(F32)
                    for j in range(4):
                        p0 = (4 * (u % 2) + j) * P
                        i = nc.tensor.transpose(ps[2 + u % 2][:, j * P:(j + 1) * P], a[:, p0:p0 + P], idf[:, :])
                    i.then_inc(tr2, 1)

            def raw_scores(o, q, k):
                for t in range(2):
                    mm(o[:, t * S:(t + 1) * S], q[:, t * P:(t + 1) * P], k, True, False)
                    i = mm(o[:, 3 * P * t:3 * P * t + P], idb[:, :], maskb[:, 0, :], False, True)
                return i

            def max1(b):
                def head(h):
                    if h == 0:
                        wait(pe, qke, 16 * b + 16)
                    if h % 2 == 0:
                        wait(pe, rrd, H // 2 * b + h // 2 + 1)
                    if h >= 2:
                        wait(pe, mx1, 16 * b + h - 1)
                    j = (h // 2 % 2, h % 2)
                    raw_scores(ps[2 + h % 2], qr[:, j[0], j[1], :], kr[:, j[0], j[1], :]).then_inc(m1d, 1)
                return head

            def max2(b):
                def head(h):
                    if h == 0:
                        wait(pe, t2e, 8 * b + 8)
                    if h >= 2:
                        wait(pe, mx2, 16 * b + h - 1)
                    raw_scores(ps[2 + h % 2], qt2[:, h, :], kt2[:, h // 2, :]).then_inc(m2d, 1)
                return head

            def heads(b, scores_t, st, ex_, pv, ov_, v, before_h0, before_pv0, max_head):
                before_h0()

                def values(g):
                    wait(pe, ex_, 16 * b + G * (g + 1))
                    if g == 0:
                        before_pv0()
                    if g >= 2:
                        wait(pe, ov_, NG * b + g - 1)
                    for k, (o0, e0, n) in enumerate(((0, P, S), (P, 0, P))):
                        for j in range(G):
                            h = G * g + j
                            i = mm(ps[6 + g % 2][PADV * j:PADV * (j + 1), o0:o0 + n], v[:, k, h, :],
                                   ex[:, h % (2 * G), e0:e0 + n], k == 0, k == 1, tile_position=(0, PADV * j))
                    i.then_inc(pv, 1)

                for h in range(H):
                    if h >= 2:
                        wait(pe, ex_, 16 * b + h - 1)
                    scores_t(h, ps[4 + h % 2]).then_inc(st, 1)
                    max_head(h)
                    if h >= G and h % G == G - 1:
                        values(h // G - 1)
                values(NG - 1)

            def scores1(h, o):
                mm(o[:, P:2 * P], kt[:, h, P:S], qt[:, h, P:S], True, False)
                mm(o[:, P:2 * P], idb[:, :], maskb[:, 1, :], False, True)
                mm(o[:, 2 * P:4 * P], kt[:, h, 0:P], qt[:, h, :], True, False)
                return mm(o[:, 2 * P:3 * P], idb[:, :], maskb[:, 1, :], False, True)

            def scores2(h, o):
                mm(o[:, 0:2 * P], kt2[:, h // 2, P:S], qt2[:, h, :], True, False)
                mm(o[:, P:2 * P], idb[:, :], maskb[:, 1, :], False, True)
                mm(o[:, 2 * P:4 * P], kt2[:, h // 2, 0:P], qt2[:, h, :], True, False)
                return mm(o[:, 2 * P:3 * P], idb[:, :], maskb[:, 1, :], False, True)

            def stage_t1(b):
                def before_h0():
                    wait(pe, ex2, 16 * b)
                    wait(pe, md1, 16 * b + 16)
                    wait(pe, v1d, 2 * b + 2)
                heads(b, scores1, st1, ex1, pv1, ov1, v1, before_h0, lambda: wait(pe, x2d, b), max2(b))

            def stage_t2(b, max_head):
                def before_h0():
                    wait(pe, ex1, 16 * b + 16)
                    wait(pe, md2, 32 * b + 32)
                    wait(pe, v2d, 2 * b + 2)
                heads(b, scores2, st2, ex2, pv2, ov2, v2, before_h0, lambda: wait(pe, sd, b + 1), max_head)

            pe.wait_ge(s_c, 16 * 4)
            pe.wait_ge(s_k, 16 * 5)
            pe.wait_ge(clear, 2)
            pe.wait_ge(cast, 2)
            pe.wait_ge(combl, N_COMB)
            pe.wait_ge(wdone, N_DIRECT)

            def batch(b, first, more):
                stage_p2(b, {} if first else dict(zip((0, 1, 3), close2(b - 1))))
                stage_t1(b)
                if more:
                    stage_p1(b + 1, dict(zip((1, 4, 7), close1(b))))
                    stage_t2(b, max1(b + 1))
                else:
                    max_t(b, negm2, mx2, mtr2)
                    for step in close1(b):
                        step()
                    stage_t2(b, lambda h: None)
                    for step in close2(b):
                        step()

            stage_p1(0, {})
            for h in range(H):
                max1(0)(h)
            batch(0, True, True)
            with pe.Fori(1, last) as b:
                batch(b, False, True)
            batch(last, False, False)

            pe.wait_ge(x2d, B)
            def route(i):
                for s in range(4):
                    wait(pe, xb2d, 4 * i + s + 1)
                    wait(pe, ytd, 4 * (i - 1) + s + 1)
                    for e in range(ET):
                        t = nc.tensor.transpose(ps[s][:, e * P:(e + 1) * P], xb2[:, s, e * P:(e + 1) * P], idf[:, :])
                    t.then_inc(tr3, 1)
                for s in range(4):
                    wait(pe, ytd, 4 * i + s + 1)
                    wait(pe, lgk, 4 * (i - 1) + s + 1)
                    for e in range(ET):
                        t = mm(ps[4 + s][:, 0:NE], yt[:, s, e, :], wr[:, e, :], e == 0, e == ET - 1)
                    t.then_inc(lgd, 1)

            route(0)
            with pe.Fori(1, TT // 4) as i:
                route(i)

            def gate_up(e, s, c, it):
                n = 16 * e + 4 * c + it
                pe.wait_ge(weld, e + 1)
                for w0, bank, done, free in ((WG, 0, gd, sgd), (WU, 2, ud, hfd)):
                    wait(pe, free, n - 1)
                    k = 0
                    for wt, xt in ((weh, x2h), (wel, x2h), (weh, x2l)):
                        for m in range(ET):
                            a = wt[:, s, w0 + m * FF + it * P:w0 + m * FF + (it + 1) * P]
                            i = mm(ps[bank + it % 2][:, :], a, xt[:, m, bass.ds(c * TC, TC)], k == 0, k == 5)
                            k += 1
                    i.then_inc(done, 1)

            def down(e, s, c, it):
                n = 16 * e + 4 * c + it
                pe.wait_ge(hld, n + 1)
                if it == 0:
                    wait(pe, yd, 4 * e + c)
                for t in range(TC // P):
                    o = ps[4 + t // 2][:, (t % 2) * E:(t % 2 + 1) * E]
                    for k, (a, m) in enumerate(((hh, weh), (hh, wel), (hl, weh))):
                        i = mm(o, a[:, it % 2, t * P:(t + 1) * P], m[:, s, WD + it * E:WD + (it + 1) * E],
                               it == 0 and k == 0 and t % 2 == 0, it == IT - 1 and k == 2)
                i.then_inc(dd, 1)

            def expert(e, s, first, final):
                def chunk(c, nxt):
                    for it in range(1, IT):
                        gate_up(e, s, c, it)
                        down(e, s, c, it - 1)
                    nxt()
                    down(e, s, c, IT - 1)
                if first:
                    chunk(0, lambda: gate_up(e, s, 1, 0))
                with pe.Fori(1 if first else 0, NC - 1) as c:
                    chunk(c, lambda: gate_up(e, s, c + 1, 0))
                chunk(NC - 1, (lambda: None) if final else (lambda: gate_up(e + 1, 1 - s, 0, 0)))

            pe.wait_ge(x2ld, TT)
            pe.wait_ge(lgk, TT)
            gate_up(0, 0, 0, 0)
            expert(0, 0, True, False)
            expert(1, 1, False, False)
            with pe.Fori(1, NE // 2 - 1) as i:
                for s in range(2):
                    expert(2 * i + s, s, False, False)
            expert(NE - 2, 0, False, False)
            expert(NE - 1, 1, False, True)

        @block.scalar
        def _(act):
            def copy(o, a):
                return nc.scalar.activation(o, a, ACT.Copy)

            for j in range(2):
                t = slice(TT // 2 * j, TT // 2 * (j + 1))
                act.dma_start(xn[:, t, :], x.rearrange("(t p) e -> p t e", p=P)[:, t, :]).then_inc(s_x[j], 16)
                if j == 0:
                    for dst, src in ((idf[:, :], ident), (mask_f[:, 0, :], mask), (mask_f[:, 1, :], mask_t),
                                     (cos_t[:, :, :], cosines), (sin_t[:, :, :], sines)):
                        act.dma_start(dst, src).then_inc(s_k, 16)

            w = 0
            for m in range(ET):
                for c in range(NG + 1):
                    act.wait_ge(comb, w + 1)
                    o = ps[w % 8]
                    if c < NG:
                        copy(wh[:, m, QC + c * CH:QC + (c + 1) * CH], o[:, 0:CH]).then_inc(combh, 1)
                    else:
                        copy(wh[:, m, KC:VC].rearrange("p (h c) -> p h c", h=H)[:, :, RD:HW],
                             o[:, 0:H * D].rearrange("p (h c) -> p h c", h=H))
                        copy(wh[:, m, VC:VC + H * D], o[:, H * D:2 * H * D]).then_inc(combh, 1)
                    w += 1
            act.wait_ge(s_w, 16 * 2)
            for m in range(ET):
                copy(rope_part(wh, m), w_cols_raw[:, m, 0:H * RD].rearrange("p (h c) -> p h c", h=H)).then_inc(wfh, 1)
            for m in range(ET):
                nc.scalar.activation(wh[:, m, Q2C:WC], w_cols_raw[:, m, H * RD:], ACT.Copy,
                                     scale=ln1[:, m:m + 1]).then_inc(wfh, 1)
            act.wait_ge(s_k, 16 * 5)
            copy(idb[:, :], idf[:, :]).then_inc(cast, 1)
            copy(maskb[:, :, :], mask_f[:, :, :]).then_inc(cast, 1)

            def max_t(b, mt, mtr, md, mte, k):
                wait(act, mtr, b + 1)
                wait(act, md, k * b)
                copy(mt[:, :], ps[2][0:H, 0:S]).then_inc(mte, 1)

            def keep_back(b, fb, of_, od):
                wait(act, fb, b + 1)
                copy(otf[:, :, :].rearrange("p e t -> p (e t)"), ps[6][:, :]).then_inc(of_, 1)

            def stage_p1(b, after):
                wait(act, tr0, b + 1)
                wait(act, p2d, 4 * b)
                copy(xth[:, :, :].rearrange("p e t -> p (e t)"), ps[3][:, :]).then_inc(xthd, 1)
                if not isinstance(b, int) or b > 0:
                    max_t(b - 1, mt2, mtr2, md2, mte2, 32)
                wait(act, st1, 16 * b)
                wait(act, pv1, NG * b)

                def step_proj(i):
                    if i % 9 == 8:
                        wait(act, p1d, 18 * b + i + 1)
                        copy(v1[:, i // 9, :, 0:D],
                             ps[i % 2][:, 0:H * D].rearrange("p (h c) -> p h c", h=H)).then_inc(v1d, 1)

                def step_tr(i, n):
                    wait(act, tr1, 16 * b + n + 1)
                    g, tt = n % 8 // 2, n // 8
                    copy((qt, kt)[n % 2][:, G * g:G * (g + 1), tt * P:(tt + 1) * P],
                         ps[2 + n % 2][:, :].rearrange("p (h t) -> p h t", h=G)).then_inc(qke, 1)

                order(step_proj, step_tr, after)

            def stage_p2(b, after):
                max_t(b, mt1, mtr1, md1, mte1, 16)
                wait(act, rbd, b + 1)
                wait(act, pv2, NG * b)
                for tt in range(2):
                    r = rb[:, tt:tt + 1]
                    wait(act, p2d, 4 * b + 2 * tt + 1)
                    wait(act, s2d, 2 * b + tt)
                    nc.scalar.activation(y2[:, :, :, :].rearrange("p a h c -> p (a h c)"), ps[0][:, :],
                                         ACT.Copy, scale=r).then_inc(y2d, 1)
                    wait(act, p2d, 4 * b + 2 * tt + 2)
                    nc.scalar.activation(v2[:, tt, :, 0:D], ps[1][:, 0:H * D].rearrange("p (h c) -> p h c", h=H),
                                         ACT.Copy, scale=r).then_inc(v2d, 1)
                    if tt == 0:
                        after()
                wait(act, st2, 16 * b)
                for u in range(8):
                    wait(act, tr2, 8 * b + u + 1)
                    t = slice(u // 4 * P, (u // 4 + 1) * P)
                    a = ps[2 + u % 2][:, :].rearrange("p (h t) -> p h t", h=4)
                    if u % 4 < 2:
                        h0 = 8 * (u % 2)
                        copy(qt2[0:ST, h0:h0 + 8:2, t], a[0:ST, :, :])
                        copy(qt2[ST:P, h0 + 1:h0 + 8:2, t], a[ST:P, :, :]).then_inc(t2e, 1)
                    else:
                        copy(kt2[:, 4 * (u % 2):4 * (u % 2) + 4, t], a).then_inc(t2e, 1)

            def exps(b, st, ex_, pv, ov_, pv_before, fa_before, scale):
                pv_before()

                def keep(g):
                    if g == 0:
                        fa_before()
                    wait(act, pv, NG * b + g + 1)
                    copy(ov[:, g, :], ps[6 + g % 2][:, 0:S]).then_inc(ov_, 1)

                for h in range(H):
                    g = h // G
                    wait(act, st, 16 * b + h + 1)
                    if h % G == 0 and g >= 2:
                        wait(act, pv, NG * b + g - 1)
                    nc.scalar.activation(ex[:, h % (2 * G), :], ps[4 + h % 2][:, P:4 * P], ACT.Exp,
                                         scale=scale).then_inc(ex_, 1)
                    if h in (9, 13):
                        keep((h - 9) // G)
                keep(2)
                keep(3)

            act.wait_ge(clear, 2)
            act.wait_ge(wdone, N_DIRECT)

            def batch(b, first, more):
                stage_p2(b, (lambda: None) if first else (lambda: keep_back(b - 1, fb2, of2, o2)))
                exps(b, st1, ex1, pv1, ov1, lambda: wait(act, pv2, NG * b), lambda: wait(act, fa2, b),
                     float(HW) ** -0.5)
                if more:
                    stage_p1(b + 1, {4: lambda: keep_back(b, fb1, of1, o1)})
                else:
                    max_t(b, mt2, mtr2, md2, mte2, 32)
                    keep_back(b, fb1, of1, o1)
                exps(b, st2, ex2, pv2, ov2, lambda: wait(act, pv1, NG * b + NG), lambda: wait(act, fa1, b + 1),
                     float(D) ** -0.5)
                if not more:
                    keep_back(b, fb2, of2, o2)

            stage_p1(0, {})
            batch(0, True, True)
            with act.Fori(1, last) as b:
                batch(b, False, True)
            batch(last, False, False)

            def scaled(i):
                for s in range(4):
                    wait(act, tr3, 4 * i + s + 1)
                    wait(act, lgd, 4 * (i - 1) + s + 1)
                    wait(act, x2ld, 4 * (i - 1) + s + 1)
                    for e in range(ET):
                        a = nc.scalar.activation(yt[:, s, e, :], ps[s][:, e * P:(e + 1) * P], ACT.Copy,
                                                 scale=ln2[:, e:e + 1])
                    a.then_inc(ytd, 1)

            scaled(0)
            with act.Fori(1, TT // 4) as i:
                scaled(i)
            act.wait_ge(gch, 1)
            nc.scalar.activation(gate[:, 1, :], gate[:, 0, :], ACT.Exp).then_inc(gex, 1)

            def silus(n):
                for it in range(IT):
                    wait(act, gd, 4 * n + it + 1)
                    wait(act, hfd, 4 * n + it - 1)
                    nc.scalar.activation(sg[:, it % 2, :], ps[it % 2][:, :], ACT.Silu).then_inc(sgd, 1)

            silus(0)
            with act.Fori(1, NE * NC) as n:
                silus(n)

            for j in range(TT // 4):
                act.wait_ge(yd, NE * NC - (TT // 4) + j + 1)
                act.wait_ge(mud, j)
                nc.scalar.activation(gl[:, :, :], xn[:, 4 * j:4 * j + 4, :], ACT.Silu).then_inc(gld, 1)

        @block.vector
        def _(dve):
            def copy(o, a):
                return nc.vector.tensor_copy(o, a)

            def minus(o, a, b):
                return nc.vector.tensor_tensor(o, a, b.bitcast(F32), ALU.subtract)

            for j in range(2):
                dve.wait_ge(s_x[j], 16)
                with dve.Fori(TT // 8 * j, TT // 8 * (j + 1)) as i:
                    for t in range(4):
                        nc.vector.bn_stats(stats[:, bass.ds(4 * i + t, 1), :].rearrange("p o c -> p (o c)"),
                                           xn[:, bass.ds(4 * i + t, 1), :].rearrange("p o e -> p (o e)")
                                           ).then_inc(st_a, 1)
            dve.wait_ge(st_a, TT)
            for t in range(TT):
                nc.vector.bn_aggr(mv[:, t, :], stats[:, t, :]).then_inc(st_b, 1)
            dve.wait_ge(st_b, TT)
            nc.vector.tensor_scalar(msq[:, :], mv[:, :, 1], EPS, None, ALU.add).then_inc(st_b, 1)

            w = 0
            for m in range(ET):
                for c in range(NG + 1):
                    dve.wait_ge(combh, w + 1)
                    o = ps[w % 8]
                    if c < NG:
                        cs = slice(QC + c * CH, QC + (c + 1) * CH)
                        minus(wl[:, m, cs], o[:, 0:CH], wh[:, m, cs]).then_inc(combl, 1)
                    else:
                        kh, kl = (a[:, m, KC:VC].rearrange("p (h c) -> p h c", h=H)[:, :, RD:HW] for a in (wh, wl))
                        minus(kl, o[:, 0:H * D].rearrange("p (h c) -> p h c", h=H), kh)
                        cs = slice(VC, VC + H * D)
                        minus(wl[:, m, cs], o[:, H * D:2 * H * D], wh[:, m, cs]).then_inc(combl, 1)
                    w += 1
            for m in range(ET):
                dve.wait_ge(wfh, m + 1)
                minus(rope_part(wl, m), w_cols_raw[:, m, 0:H * RD].rearrange("p (h c) -> p h c", h=H),
                      rope_part(wh, m)).then_inc(wdone, 1)

            dve.wait_ge(powd, 1)
            with dve.Fori(0, TT // 4) as j:
                for t in range(4):
                    a = xn[:, bass.ds(4 * j + t, 1), :].rearrange("p o e -> p (o e)")
                    nc.vector.tensor_scalar(a, a, mv[:, bass.ds(4 * j + t, 1), 0], rstd[:, bass.ds(4 * j + t, 1)],
                                            ALU.subtract, ALU.mult).then_inc(xnd, 1)
            nc.vector.tensor_tensor(msq[:, :], mv[:, :, 1], rstd[:, :], ALU.mult).then_inc(msd, 1)
            dve.wait_ge(msd, 1)
            nc.vector.tensor_tensor(msq[:, :], msq[:, :], rstd[:, :], ALU.mult).then_inc(msd, 1)
            dve.wait_ge(msd, 2)
            nc.vector.tensor_scalar(msq[:, :], msq[:, :], EPS, None, ALU.add).then_inc(msd, 1)

            for m in range(ET):
                dve.wait_ge(wfh, ET + m + 1)
                nc.vector.scalar_tensor_tensor(out=wl[:, m, Q2C:WC], in0=w_cols_raw[:, m, H * RD:],
                                               scalar=ln1[:, m:m + 1], in1=wh[:, m, Q2C:WC].bitcast(F32),
                                               op0=ALU.mult, op1=ALU.subtract).then_inc(wdone, 1)

            def copy_batch(b):
                wait(dve, tr0, b)
                copy(xb[:, :, :], xn[:, bass.ds(2 * b, 2), :]).then_inc(xbd, 1)

            def copy_rms1(b):
                wait(dve, v2d, 2 * b)
                copy(rb[:, :], rms1[:, bass.ds(2 * b, 2)]).then_inc(rbd, 1)

            def close_heads(b, fa, rc, on_, od, keep):
                def normalise():
                    wait(dve, fa, b + 1)
                    for tt in range(2):
                        a = ps[6 + tt][:, :].rearrange("p (h c) -> p h c", h=H)
                        i = nc.vector.reciprocal(rec[:, tt, :], a[:, :, V1])
                    i.then_inc(rc, 1)
                    wait(dve, rc, b + 1)
                    for tt in range(2):
                        a = ps[6 + tt][:, :].rearrange("p (h c) -> p h c", h=H)
                        i = nc.vector.tensor_tensor(otk[:, tt, :, :], a[:, :, 0:D],
                                                    rec[:, tt, :].unsqueeze(2).broadcast_to([P, H, D]), ALU.mult)
                    i.then_inc(on_, 1)

                def kept():
                    wait(dve, od, b + 1)
                    keep(b)
                return normalise, kept

            def keep_s(b):
                wait(dve, sst, 16 * b)
                copy(s_b[:, :, :].rearrange("p t e -> p (t e)"), ps[7][:, :]).then_inc(sd, 1)

            def keep_x2(b):
                a = xn[:, bass.ds(2 * b, 2), :]
                nc.vector.tensor_tensor(a, ps[7][:, :].rearrange("p (t e) -> p t e", t=2), a, ALU.add).then_inc(x2d, 1)

            def close1(b):
                return close_heads(b, fa1, rc1, on1, o1, keep_s)

            def close2(b):
                return close_heads(b, fa2, rc2, on2, o2, keep_x2)

            def stage_p1(b, after):
                wait(dve, xthd, b + 1)
                minus(xtl[:, :, :].rearrange("p e t -> p (e t)"), ps[3][:, :],
                      xth[:, :, :].rearrange("p e t -> p (e t)")).then_inc(xtld, 1)
                for n in range(16):
                    tt = n // 8
                    i = 9 * tt + n % 8
                    wait(dve, p1d, 18 * b + i + 1)
                    wait(dve, tr1, 16 * b + max(n - 3, 0))
                    wait(dve, tokd, 16 * b + max(n - 1, 0))
                    a = ps[i % 2][:, 0:CH].rearrange("p (h c) -> p h c", h=G)
                    nc.vector.tensor_tensor(tok[:, n % 4, :, 0:HW], a,
                                            cos_t[:, tt:tt + 1, :].broadcast_to([P, G, HW]), ALU.mult)
                    sw = a[:, :, 0:RD].rearrange("p h (s d) -> p h s d", s=2)[:, :, ::-1, :]
                    sn = sin_t[:, tt:tt + 1, :].broadcast_to([P, G, RD]).rearrange("p h (s d) -> p h s d", s=2)
                    nc.vector.tensor_tensor(swp[:, n % 2, :, :].rearrange("p h (s d) -> p h s d", s=2), sw, sn,
                                            ALU.mult).then_inc(roped, 1)
                    after.get(n, lambda: None)()

            def stage_m1(b):
                wait(dve, qke, 16 * b + 16)
                wait(dve, mtr1, b)

                def rounded(g):
                    wait(dve, m1d, 16 * b + 2 * max(g - 1, 0))
                    copy(qr[:, g % 2, :, :], qt[:, 2 * g:2 * g + 2, :])
                    copy(kr[:, g % 2, :, :], kt[:, 2 * g:2 * g + 2, :]).then_inc(rrd, 1)

                rounded(0)
                for h in range(H):
                    if h % 2 == 0 and h + 2 < H:
                        rounded(h // 2 + 1)
                    maxima(b, h, h, negm1, m1d, mx1)

            def stage_m2(b):
                wait(dve, mtr2, b)
                for h in range(H):
                    maxima(b, h, (h % 2) * (H // 2) + h // 2, negm2, m2d, mx2)

            def maxima(b, h, col, negm, md, mx):
                wait(dve, md, 16 * b + h + 1)
                o = ps[2 + h % 2]
                nc.vector.tensor_reduce(negm[:, 0, col:col + 1], o[:, 0:P], AX.X, ALU.max, negate=True)
                nc.vector.tensor_reduce(negm[:, 1, col:col + 1], o[:, S:2 * S], AX.X, ALU.max,
                                        negate=True).then_inc(mx, 1)

            def stage_p2(b, after):
                for tt in range(2):
                    wait(dve, y2d, 2 * b + tt + 1)
                    wait(dve, tr2, 8 * b + 4 * tt)
                    q, k = y2[:, 0, :, :], y2[:, 1, :, :]
                    copy(qs[:, :, 0:D], q)
                    copy(qs[:, :, D:2 * D], q)
                    copy(ks[:, :, 0:D], k)
                    copy(ks[:, :, 2 * D:3 * D], k).then_inc(hi2, 1)
                    wait(dve, hi2, 2 * b + tt + 1)
                    minus(qs[:, :, 2 * D:3 * D], q, qs[:, :, 0:D])
                    minus(ks[:, :, D:2 * D], k, ks[:, :, 0:D]).then_inc(s2d, 1)
                    after.get(tt, lambda: None)()

            def batch(b, first, more):
                stage_p2(b, {} if first else dict(enumerate(close2(b - 1))))
                stage_m2(b)
                if more:
                    copy_batch(b + 1)
                    copy_rms1(b + 1)
                    normalise, kept = close1(b)
                    stage_p1(b + 1, {1: normalise, 7: kept})
                    stage_m1(b + 1)
                else:
                    for step in (*close1(b), *close2(b)):
                        step()

            dve.wait_ge(xnd, TT)
            dve.wait_ge(clear, 2)
            copy_batch(0)
            stage_p1(0, {})
            dve.wait_ge(rmd, 1)
            copy_rms1(0)
            stage_m1(0)
            batch(0, True, True)
            with dve.Fori(1, last) as b:
                batch(b, False, True)
            batch(last, False, False)

            def split_expert(e, s):
                wait(dve, rawd[s], 8 * e + 16 - 8 * s)
                wait(dve, dd, 16 * (e - 1))
                copy(weh[:, s, :], raw[:, s, :]).then_inc(wehd, 1)
                wait(dve, wehd, e + 1)
                minus(wel[:, s, :], raw[:, s, :], weh[:, s, :]).then_inc(weld, 1)

            dve.wait_ge(x2d, B)
            with dve.Fori(0, TT // 4) as j:
                for t in range(4):
                    nc.vector.bn_stats(stats[:, bass.ds(4 * j + t, 1), :].rearrange("p o c -> p (o c)"),
                                       xn[:, bass.ds(4 * j + t, 1), :].rearrange("p o e -> p (o e)")).then_inc(st_a, 1)
            dve.wait_ge(st_a, 2 * TT)
            for t in range(TT):
                nc.vector.bn_aggr(mv[:, t, :], stats[:, t, :]).then_inc(st_c, 1)
            dve.wait_ge(st_c, TT)
            nc.vector.tensor_tensor(msq[:, :], mv[:, :, 0], mv[:, :, 0], ALU.mult).then_inc(ms2, 1)
            dve.wait_ge(ms2, 1)
            nc.vector.scalar_tensor_tensor(out=msq[:, :], in0=msq[:, :], scalar=EPS, in1=mv[:, :, 1],
                                           op0=ALU.add, op1=ALU.add).then_inc(ms2, 1)
            split_expert(0, 0)
            dve.wait_ge(rm2, 1)
            def scale_tokens(i):
                for s in range(4):
                    wait(dve, tr3, 4 * (i - 1) + s + 1)
                    nc.vector.tensor_scalar(xb2[:, s, :], xn[:, bass.ds(4 * i + s, 1), :].rearrange("p o e -> p (o e)"),
                                            rstd[:, bass.ds(4 * i + s, 1)], None, ALU.mult).then_inc(xb2d, 1)

            def keep_columns(i):
                for s in range(4):
                    wait(dve, ytd, 4 * i + s + 1)
                    t = bass.ds((4 * i + s) * P, P)
                    copy(x2h[:, :, t], yt[:, s, :, :]).then_inc(x2hd, 1)
                    wait(dve, x2hd, 4 * i + s + 1)
                    minus(x2l[:, :, t], yt[:, s, :, :], x2h[:, :, t]).then_inc(x2ld, 1)
                for s in range(4):
                    wait(dve, lgd, 4 * i + s + 1)
                    copy(lg[:, bass.ds(4 * i + s, 1), :].rearrange("p o n -> p (o n)"),
                         ps[4 + s][:, 0:NE]).then_inc(lgk, 1)

            scale_tokens(0)
            with dve.Fori(1, TT // 4) as i:
                scale_tokens(i)
                keep_columns(i - 1)
            keep_columns(TT // 4 - 1)

            def top_two(tiles):
                for t in tiles:
                    nc.vector.max(mx[:, t, :], lg[:, t, :]).then_inc(top, 1)
                    dve.wait_ge(top, 2 * t + 1)
                    nc.vector.max_index(ix[:, t, :], mx[:, t, :], lg[:, t, :]).then_inc(top, 1)

            def gates():
                dve.wait_ge(top, 2 * TT)
                nc.vector.tensor_tensor(gate[:, 0, :], mx[:, :, 1], mx[:, :, 0], ALU.subtract).then_inc(gch, 1)
                copy(ixf[:, :, :], ix[:, :, 0:2])
                dve.wait_ge(gch, 1)
                dve.wait_ge(gex, 1)
                nc.vector.tensor_scalar(gate[:, 0, :], gate[:, 1, :], 1.0, None, ALU.add).then_inc(gch, 1)
                dve.wait_ge(gch, 2)
                nc.vector.reciprocal(gate[:, 2, :], gate[:, 0, :]).then_inc(gch, 1)
                dve.wait_ge(gch, 3)
                nc.vector.tensor_tensor(gate[:, 3, :], gate[:, 1, :], gate[:, 2, :], ALU.mult).then_inc(gch, 1)
                dve.wait_ge(gch, 4)
                dve.wait_ge(xrd, 48)
                for j in range(2):
                    nc.vector.tensor_tensor(pick[:, j, :, :], iot[:, :, :],
                                            ixf[:, :, j:j + 1].broadcast_to([P, TT, NE]), ALU.is_equal).then_inc(gch, 1)
                    dve.wait_ge(gch, 5 + 2 * j)
                    nc.vector.tensor_tensor(pick[:, j, :, :], pick[:, j, :, :],
                                            gate[:, 2 + j, :].unsqueeze(2).broadcast_to([P, TT, NE]),
                                            ALU.mult).then_inc(gch, 1)
                    dve.wait_ge(gch, 6 + 2 * j)
                nc.vector.tensor_tensor(cw[:, :, :].rearrange("p n t -> p t n"), pick[:, 0, :, :], pick[:, 1, :, :],
                                        ALU.add).then_inc(cwd, 1)
                dve.wait_ge(cwd, 1)

            def product(n, it):
                dve.wait_ge(ud, n + 1)
                dve.wait_ge(sgd, n + 1)
                nc.vector.tensor_tensor(hf[:, it % 2, :], ps[2 + it % 2][:, :], sg[:, it % 2, :],
                                        ALU.mult).then_inc(hfd, 1)
                dve.wait_ge(hfd, n + 1)
                copy(hh[:, it % 2, :], hf[:, it % 2, :]).then_inc(hhd, 1)
                dve.wait_ge(hhd, n + 1)
                minus(hl[:, it % 2, :], hf[:, it % 2, :], hh[:, it % 2, :]).then_inc(hld, 1)

            def add_y(e, c):
                dve.wait_ge(dd, 16 * e + 4 * c + 4)
                for t in range(TC // P):
                    a = xn[:, bass.ds(4 * c + t, 1), :].rearrange("p o e -> p (o e)")
                    w_ = cw[:, bass.ds(e, 1), bass.ds(4 * c + t, 1)].rearrange("p a b -> p (a b)")
                    i = nc.vector.scalar_tensor_tensor(out=a, in0=ps[4 + t // 2][:, (t % 2) * E:(t % 2 + 1) * E],
                                                       scalar=w_, in1=a, op0=ALU.mult, op1=ALU.add)
                i.then_inc(yd, 1)

            def expert(e, s, final):
                def chunk(c, n):
                    for it in range(1, IT):
                        product(n + it, it)
                    if not (final and isinstance(c, int)):
                        product(n + IT, 0)
                    add_y(e, c)
                if not final:
                    chunk(0, 16 * e)
                    split_expert(e + 1, 1 - s)
                    with dve.Fori(1, NC) as c:
                        chunk(c, 16 * e + 4 * c)
                else:
                    with dve.Fori(0, NC - 1) as c:
                        chunk(c, 16 * e + 4 * c)
                    chunk(NC - 1, 16 * e + 4 * (NC - 1))

            top_two(range(TT))
            gates()
            product(0, 0)
            expert(0, 0, False)
            expert(1, 1, False)
            with dve.Fori(1, NE // 2 - 1) as i:
                for s in range(2):
                    expert(2 * i + s, s, False)
            expert(NE - 2, 0, False)
            expert(NE - 1, 1, True)

            for j in range(TT // 4):
                t = slice(4 * j, 4 * j + 4)
                dve.wait_ge(gld, j + 1)
                nc.vector.tensor_tensor(s_tok[:, t, :], s_tok[:, t, :], gl[:, :, :], ALU.mult).then_inc(mud, 1)
                dve.wait_ge(mud, j + 1)
                nc.vector.tensor_tensor(xr[:, t, :], xr[:, t, :], s_tok[:, t, :], ALU.add).then_inc(fin, 1)


def laid_out(f):
    a = {k: np.asarray(v) for k, v in f.items()}
    dt = np.float32

    def per_head(w, rows):
        return w.reshape(H, rows, w.shape[1])

    w_uqr = np.concatenate([per_head(a["L0_attn_w_qr"], RD), per_head(a["L0_attn_w_uq"], D)], 1).reshape(H * HW, CQ).T
    w_ukv = np.concatenate([a["L0_attn_w_uk"], a["L0_attn_w_uv"]], 0).T
    w_cols = np.concatenate([a["L0_attn_w_kr"], a["L0_ffn_Wq"], a["L0_ffn_Wk"], a["L0_ffn_Wv"]], 0).T

    def lhs(w):
        return w.T.reshape(ET, P, FF).transpose(1, 0, 2).reshape(P, ET * FF)

    experts = np.stack([np.concatenate([
        lhs(a["L0_ffn_Wg"][e]), lhs(a["L0_ffn_Wu"][e]),
        a["L0_ffn_Wd"][e].T.reshape(IT, P, E).transpose(1, 0, 2).reshape(P, IT * E)], 1) for e in range(NE)])

    pos = np.arange(S, dtype=dt)
    inv = (1.0 / 10000.0 ** (np.arange(0, RD, 2, dtype=dt) / RD)).astype(dt)
    ang = (pos[:, None] * inv[None, :]).astype(dt)
    c, s = np.cos(ang), np.sin(ang)
    cosines = np.concatenate([c, c, np.ones((S, D), dt)], 1).reshape(2, P, HW).transpose(1, 0, 2)
    sines = np.concatenate([-s, s], 1).reshape(2, P, RD).transpose(1, 0, 2)
    i = np.arange(P)
    mask = np.where(i[None, :] > i[:, None], BIG, 0.0)
    consts = dict(cosines=cosines, sines=sines, ident=np.eye(P), mask=mask, mask_t=mask.T,
                  experts_iota=np.broadcast_to(np.arange(NE), (P, TT, NE)))
    r = dict(
        x=a["L0_attn_x"].reshape(T, E), w_cols=w_cols, w_dq=a["L0_attn_w_dq"], w_uqr=w_uqr,
        w_dkv=a["L0_attn_w_dkv"], w_ukv=w_ukv, w_out=a["L0_attn_w_out"].T, w_o=a["L0_ffn_Wo"].T,
        w_ln1=a["L0_ffn_w_ln1"].reshape(ET, P).T, w_ln2=a["L0_ffn_w_ln2"].reshape(ET, P).T,
        w_r=a["L0_ffn_Wr"].T, w_experts=experts, **{k: v.astype(dt) for k, v in consts.items()})
    return {k: np.ascontiguousarray(v) for k, v in r.items()}


def kernel(**inputs):
    import concourse.bacc as bacc
    from concourse.bass_utils import run_bass_kernel_spmd

    nc = bacc.Bacc("TRN2", target_bir_lowering=False, num_devices=1)
    arrays = laid_out(inputs)
    args = {k: nc.dram_tensor(f"in_{k}", v.shape, mybir.dt.from_np(v.dtype), kind="ExternalInput").ap()
            for k, v in arrays.items()}
    out = nc.dram_tensor("out_0", (T, E), F32, kind="ExternalOutput").ap()
    build(nc, out=out, **args)
    r = run_bass_kernel_spmd(nc, [{f"in_{k}": v for k, v in arrays.items()}], core_ids=[0])
    return r.results[0]["out_0"].reshape(B, S, E)
```

```python
from contextlib import ExitStack

import numpy as np

import concourse.bass as bass
from concourse import mybir

F32 = mybir.dt.float32
F32R = mybir.dt.float32r
BF16 = mybir.dt.bfloat16
U32 = mybir.dt.uint32
ALU = mybir.AluOpType
ACT = mybir.ActivationFunctionType
AX = mybir.AxisListType

P = 128
B, S, E = 8, 256, 256
H, D, RD = 16, 16, 64
CQ, CKV = 192, 64
RT = CQ // 2
NE, FF = 8, 512
T = B * S
TT = T // P
ET = E // P
HW = RD + D
MROW = HW
G = 4
NG = H // G
PADV = 32
ST = 64
MROW2 = 3 * D
V1 = D
QC, KC, VC = 0, H * HW, 2 * H * HW
Q2C = VC + H * D
V2C = Q2C + 2 * H * D
WC = V2C + H * D
CH = G * HW
EPS = 1e-5
BIG = -1e30
BOUND = 1e30
IT = FF // P
TC = 512
NC = T // TC
WG, WU, WD = 0, ET * FF, 2 * ET * FF
WE = WD + IT * E


def wait(engine, semaphore, value):
    if not isinstance(value, int) or value > 0:
        engine.wait_ge(semaphore, value)


def build(nc, x, w_cols, w_dq, w_uqr, w_dkv, w_ukv, w_out, w_o, w_ln1, w_ln2, w_r, w_experts,
          cosines, sines, ident, mask, mask_t, seen_t, experts_iota, out):
    ctx = ExitStack()
    with ctx:
        def sb(name, shape, dt=F32, stack=ctx):
            return stack.enter_context(nc.sbuf_tensor(name, shape, dt))

        def sem(name):
            return ctx.enter_context(nc.semaphore(name))

        xn = sb("xn", [P, TT, E])
        s_dram = nc.dram_tensor("mla_branch", (T, E), F32).ap()
        s_view = s_dram.rearrange("(t p) e -> p t e", p=P)
        idf = sb("idf", [P, P])
        ln2 = sb("ln2", [P, ET])
        wr = sb("wr", [P, ET, NE])
        rms1 = sb("rms1", [P, TT])
        mv = sb("mv", [P, TT, 2])
        stats = sb("stats", [P, TT, 6])
        msq = sb("msq", [P, TT])
        rstd = sb("rstd", [P, TT])
        mhalf = sb("mhalf", [P, TT])

        early = ExitStack()
        late = ExitStack()
        cos_t = sb("cos_t", [P, ET, HW], F32, early)
        sin_t = sb("sin_t", [P, ET, RD], F32, early)
        wh = sb("wh", [P, ET, WC], F32R, early)
        wl = sb("wl", [P, ET, WC], F32R, early)
        ln1 = sb("ln1", [P, ET], F32, early)
        xb = sb("xb", [P, 2, E], F32, early)
        rb = sb("rb", [P, 2], F32, early)
        xth = sb("xth", [P, ET, S], F32R, early)
        xtl = sb("xtl", [P, ET, S], F32R, early)
        tok = sb("tok", [P, 4, G, P], F32, early)
        swp = sb("swp", [P, 2, G, RD], F32, early)
        qr = sb("qr", [P, 2, 2, S], F32R, early)
        kr = sb("kr", [P, 2, 2, S], F32R, early)
        qs = sb("qs", [P, 2, H, ST], F32R, early)
        ks = sb("ks", [P, 2, H, ST], F32R, early)
        v1 = sb("v1", [P, 2, H, PADV], F32, early)
        negm1 = sb("negm1", [P, 2, H], F32, early)
        prep = ExitStack()
        mask_f = sb("mask_f", [P, 2, P], F32, prep)
        w_cols_raw = sb("w_cols_raw", [P, ET, H * RD + 3 * E], F32, prep)
        w_uqr_raw = sb("w_uqr_raw", [P, 2, H * HW], F32, prep)
        w_dq_raw = sb("w_dq_raw", [P, 2, E], F32, prep)
        w_dkv_raw = sb("w_dkv_raw", [CKV, E], F32, prep)
        w_ukv_raw = sb("w_ukv_raw", [CKV, 2 * H * D], F32, prep)
        prep.close()
        qt = sb("qt", [P, H, S], F32, early)
        kt = sb("kt", [P, H, S], F32, early)

        seen = sb("seen", [P, 1, P], F32, late)
        idb = sb("idb", [P, P], BF16, late)
        maskb = sb("maskb", [P, 2, P], BF16, late)
        wo1 = sb("wo1", [P, ET, E], F32, late)
        wo2 = sb("wo2", [P, ET, E], F32, late)
        qt2 = sb("qt2", [P, H, S], F32R, late)
        kt2 = sb("kt2", [P, H // 2, S], F32R, late)
        v2 = sb("v2", [P, 2, H, PADV], F32, late)
        ex = sb("ex", [P, 2 * G, 3 * P], F32, late)
        ov = sb("ov", [P, NG, S], F32, late)
        rec = sb("rec", [P, 2, H], F32, late)
        otk = sb("otk", [P, 2, H, D], F32, late)
        otf = sb("otf", [P, ET, S], F32, late)
        s_b = sb("s_b", [P, 2, E], F32, late)
        negm2 = sb("negm2", [P, 2, H], F32, late)
        mt = sb("mt", [H, S], F32R, late)
        late.close()
        early.close()

        moe = ExitStack()
        raw = sb("raw", [P, 2, WE], F32, moe)
        weh = sb("weh", [P, 2, WE], F32R, moe)
        wel = sb("wel", [P, 2, WE], F32R, moe)
        x2h = sb("x2h", [P, ET, T], F32R, moe)
        x2l = sb("x2l", [P, ET, T], F32R, moe)
        xb2 = sb("xb2", [P, 2, E], F32, moe)
        yt = sb("yt", [P, 2, ET, P], F32, moe)
        lg = sb("lg", [P, TT, NE], F32, moe)
        mx = sb("mx", [P, TT, NE], F32, moe)
        ix = sb("ix", [P, TT, NE], U32, moe)
        ixf = sb("ixf", [P, TT, 2], F32, moe)
        iot = sb("iot", [P, TT, NE], F32, moe)
        gate = sb("gate", [P, 4, TT], F32, moe)
        pick = sb("pick", [P, 2, TT, NE], F32, moe)
        cw = sb("cw", [P, NE, TT], F32, moe)
        sg = sb("sg", [P, 2, TC], F32, moe)
        hf = sb("hf", [P, 2, TC], F32, moe)
        hh = sb("hh", [P, 2, TC], F32R, moe)
        hl = sb("hl", [P, 2, TC], F32R, moe)
        xr = sb("xr", [P, TT, E], F32, moe)
        s_tok = sb("s_tok", [P, TT, E], F32, moe)
        gl = sb("gl", [P, 4, E], F32, moe)
        moe.close()

        ps = [ctx.enter_context(nc.psum_tensor(f"ps{i}", [P, 512], F32)) for i in range(8)]

        s_lr = sem("low_rank_weights_loaded")
        s_w = sem("direct_weights_loaded")
        s_c = sem("late_weights_loaded")
        s_k = sem("constants_loaded")
        s_x = [sem("x_first_batch_loaded"), sem("x_first_half_loaded"), sem("x_second_half_loaded")]
        cast = sem("masks_cast")
        clear = sem("pads_set")
        comb = sem("weights_combined")
        combh = sem("combined_high")
        combl = sem("combined_low")
        wfh = sem("direct_high")
        wdone = sem("direct_low")
        wdonep = sem("rotary_low_first")
        st_a = sem("stats_taken")
        st_b = sem("stats_joined")
        powd = sem("rstd_ready")
        xnd = sem("xn_ready")
        msd = sem("mean_squares")
        rmd = sem("rms1_ready")
        xbd = sem("batch_copied")
        rbd = sem("rms1_copied")
        tr0 = sem("xT_transposed")
        xthd = sem("xT_high")
        xtld = sem("xT_low")
        p1d = sem("mla_projected")
        roped = sem("rope_products")
        tokd = sem("rope_done")
        tr1 = sem("mla_transposed")
        qke = sem("mla_qk_kept")
        v1d = sem("mla_v_kept")
        rrd = sem("mla_q_rounded")
        rkd = sem("mla_k_rounded")
        m1d = sem("mla_scores")
        mx1 = sem("mla_max")
        mtr1 = sem("mla_max_transposed")
        mte1 = sem("mla_max_kept")
        md1 = sem("mla_max_row")
        st1 = sem("mla_scores_t")
        ex1 = sem("mla_exp")
        exm1 = sem("mla_exp_masked")
        pv1 = sem("mla_pv")
        ov1 = sem("mla_heads_kept")
        fa1 = sem("mla_heads_to_tokens")
        rc1 = sem("mla_reciprocal")
        on1 = sem("mla_heads_normalised")
        fb1 = sem("mla_heads_back")
        of1 = sem("mla_heads_back_kept")
        o1 = sem("mla_out")
        sd = sem("mla_out_kept")
        sst = sem("mla_out_stored")
        p2d = sem("mha_projected")
        v2d = sem("mha_v_kept")
        hi2 = sem("mha_qk_high")
        s2d = sem("mha_qk_stacked")
        tr2 = sem("mha_transposed")
        t2e = sem("mha_qk_kept")
        t2o = sem("mha_q_odd_kept")
        m2d = sem("mha_scores")
        mx2 = sem("mha_max")
        mtr2 = sem("mha_max_transposed")
        mte2 = sem("mha_max_kept")
        md2 = sem("mha_max_row")
        st2 = sem("mha_scores_t")
        ex2 = sem("mha_exp")
        pv2 = sem("mha_pv")
        ov2 = sem("mha_heads_kept")
        fa2 = sem("mha_heads_to_tokens")
        rc2 = sem("mha_reciprocal")
        on2 = sem("mha_heads_normalised")
        fb2 = sem("mha_heads_back")
        of2 = sem("mha_heads_back_kept")
        o2 = sem("mha_out")
        x2d = sem("ffn_residual")
        st_c = sem("stats2_taken")
        st_d = sem("stats2_joined")
        ms2 = sem("mean_squares2")
        rm2 = sem("rms2_ready")
        xb2d = sem("x2_scaled")
        tr3 = sem("x2_transposed")
        ytd = sem("x2T_scaled")
        x2hd = sem("x2T_high")
        x2ld = sem("x2T_low")
        lgd = sem("router_logits")
        lgk = sem("logits_kept")
        top = sem("top2_found")
        gch = sem("gate_steps")
        gex = sem("gate_exp")
        cwd = sem("expert_weights_ready")
        rawd = [sem("expert_loaded_even"), sem("expert_loaded_odd")]
        wehd = sem("expert_high")
        weld = sem("expert_low")
        gd = sem("hg_done")
        ud = sem("hu_done")
        sgd = sem("silu_done")
        hfd = sem("h_done")
        hhd = sem("h_high")
        hld = sem("h_low")
        dd = sem("down_done")
        yd = sem("y_added")
        iotd = sem("iota_loaded")
        xrd = sem("x_again")
        gld = sem("ffn_silu")
        mud = sem("branches_multiplied")
        fin = sem("result_ready")
        s_out = sem("stored")

        last = B - 1
        N_DIRECT = 1 + ET
        N_COMB = ET * (NG + 1)
        EARLY = TT - 2
        LOADED = (slice(0, 2), slice(2, TT // 2), slice(TT // 2, TT))
        ROUTED = (slice(0, EARLY), slice(EARLY, TT))

        def normalised(t):
            return nc.vector.tensor_scalar(xn[:, t, :], xn[:, t, :], mv[:, t, 0:1], rstd[:, t:t + 1],
                                           ALU.subtract, ALU.mult)

        def bank2(u):
            return ps[(3, 2, 0)[u % 3]]

        def rope_part(w, m):
            return w[:, m, KC:VC].rearrange("p (h c) -> p h c", h=H)[:, :, 0:RD]

        block = ctx.enter_context(nc.Block())

        @block.sync
        def _(sp):
            for dst, src in ((w_dq_raw[0:RT, :, :], w_dq.rearrange("(a p) n -> p a n", p=RT)),
                             (w_uqr_raw[0:RT, :, :], w_uqr.rearrange("(a p) n -> p a n", p=RT)),
                             (w_dkv_raw[:, :], w_dkv), (w_ukv_raw[:, :], w_ukv)):
                sp.dma_start(dst, src).then_inc(s_lr, 16)
            for t, loaded in zip(LOADED, s_x):
                sp.dma_start(xn[:, t, :], x.rearrange("(t p) e -> p t e", p=P)[:, t, :]).then_inc(loaded, 16)
            for dst, src in ((w_cols_raw[:, :, :], w_cols.rearrange("(m p) n -> p m n", p=P)),
                             (ln1[:, :], w_ln1)):
                sp.dma_start(dst, src).then_inc(s_w, 16)
            for dst, src in ((ln2[:, :], w_ln2),
                             (wr[:, :, :], w_r.rearrange("(m p) n -> p m n", p=P)),
                             (wo1[:, :, :], w_out.rearrange("(m p) e -> p m e", p=P)),
                             (wo2[:, :, :], w_o.rearrange("(m p) e -> p m e", p=P))):
                sp.dma_start(dst, src).then_inc(s_c, 16)

            def row1(b):
                sp.wait_ge(mte1, b + 1)
                sp.dma_start(qt[MROW:MROW + 1, :, :], mt[:, :].bitcast(F32)).then_inc(md1, 16)

            def row2(b):
                sp.wait_ge(mte2, b + 1)
                for e in range(2):
                    r = ST * e + MROW2
                    sp.dma_start(qt2[r:r + 1, e:H:2, :].bitcast(F32),
                                 mt[e * H // 2:(e + 1) * H // 2, :].bitcast(F32)).then_inc(md2, 16)

            def store_s(b):
                sp.wait_ge(sd, b + 1)
                sp.dma_start(s_view[:, bass.ds(2 * b, 2), :], s_b[:, :, :]).then_inc(sst, 16)

            with sp.Fori(0, last) as b:
                row1(b)
                row2(b)
                store_s(b)
            row1(last)
            row2(last)

            def load(e, s):
                sp.dma_start(raw[:, s, :], w_experts[e, :, :]).then_inc(rawd[s], 16)
            sp.wait_ge(pv1, NG * B)
            load(0, 0)
            sp.dma_start(iot[:, :, :], experts_iota).then_inc(iotd, 16)
            load(1, 1)
            store_s(last)
            sp.wait_ge(x2d, B)
            sp.wait_ge(sst, 16 * B)
            sp.dma_start(xr[:, :, :], x.rearrange("(t p) e -> p t e", p=P)).then_inc(xrd, 16)
            sp.dma_start(s_tok[:, :, :], s_view).then_inc(xrd, 16)
            with sp.Fori(0, NE // 2 - 1) as i:
                for s in range(2):
                    sp.wait_ge(weld, 2 * i + s + 1)
                    sp.dma_start(raw[:, s, :],
                                 w_experts[bass.ds(2 * i + s + 2, 1), :, :].rearrange("o p n -> (o p) n")
                                 ).then_inc(rawd[s], 16)
            o_v = out.rearrange("(t p) e -> p t e", p=P)
            pieces = [slice(4 * j, 4 * j + 4) for j in range(NC - 1)] + [slice(TT - 4, TT - 2), slice(TT - 2, TT)]
            for j, t in enumerate(pieces):
                sp.wait_ge(fin, j + 1)
                sp.dma_start(o_v[:, t, :], xr[:, t, :]).then_inc(s_out, 16)
            sp.wait_ge(s_out, 16 * len(pieces))

        @block.gpsimd
        def _(pool):
            nc.gpsimd.memset(mhalf[:, :], -0.5)
            nc.gpsimd.memset(tok[:, :, :, RD:P], 0.0)
            nc.gpsimd.memset(v1[:, :, :, :], 0.0)
            nc.gpsimd.memset(v2[:, :, :, :], 0.0)
            nc.gpsimd.memset(ks[:, :, :, :].bitcast(F32), 0.0)
            nc.gpsimd.memset(qs[:, :, :, :].bitcast(F32), 0.0).then_inc(clear, 1)
            pool.wait_ge(clear, 1)
            nc.gpsimd.memset(v1[:, :, :, V1:V1 + 1], 1.0)
            nc.gpsimd.memset(v2[:, :, :, V1:V1 + 1], 1.0)
            nc.gpsimd.memset(tok[:, 1:4:2, :, MROW:MROW + 1], 1.0)
            nc.gpsimd.memset(ks[:, :, :, MROW2:MROW2 + 1].bitcast(F32), 1.0)
            nc.gpsimd.memset(qt2[:, :, :].bitcast(F32), 0.0).then_inc(clear, 1)

            def power(k, t):
                pool.wait_ge(st_b, t.stop + k + 1)
                nc.gpsimd.tensor_tensor(rstd[:, t], msq[:, t], mhalf[:, t], ALU.pow).then_inc(powd, 1)

            power(0, slice(0, 2))
            pool.wait_ge(wfh, 1)
            nc.gpsimd.tensor_tensor(rope_part(wl, 0), w_cols_raw[:, 0, 0:H * RD].rearrange("p (h c) -> p h c", h=H),
                                    rope_part(wh, 0).bitcast(F32), ALU.subtract).then_inc(wdonep, 1)
            power(1, slice(2, TT))

            def rope_sums(b):
                for n in range(2 * 2 * NG):
                    wait(pool, roped, 16 * b + n + 1)
                    t = tok[:, n % 4, :, 0:RD]
                    nc.gpsimd.tensor_tensor(t, t, swp[:, n % 2, :, :], ALU.add).then_inc(tokd, 1)

            rope_sums(0)
            pool.wait_ge(msd, 3)
            nc.gpsimd.tensor_tensor(rms1[:, :], msq[:, :], mhalf[:, :], ALU.pow).then_inc(rmd, 1)
            with pool.Fori(1, B) as b:
                rope_sums(b)
            for k, t in enumerate(ROUTED):
                pool.wait_ge(ms2, 2 * k + 2)
                nc.gpsimd.tensor_tensor(rstd[:, t], msq[:, t], mhalf[:, t], ALU.pow).then_inc(rm2, 1)

        def order(step_proj, step_tr, after):
            for i in range(2 * 9 + 2):
                if i < 18:
                    step_proj(i)
                if i >= 2 and (i - 2) % 9 != 8:
                    step_tr(i - 2, 8 * ((i - 2) // 9) + (i - 2) % 9)
                after.get(i, lambda: None)()

        @block.tensor
        def _(pe):
            def mm(o, a, m, start, stop, **k):
                return nc.tensor.matmul(o, a, m, start=start, stop=stop, skip_group_check=True, **k)

            def proj(o, c0, n, tt):
                t = slice(tt * P, (tt + 1) * P)
                k = 0
                for a, m in ((xth, wh), (xth, wl), (xtl, wh)):
                    for e in range(ET):
                        i = mm(o, a[:, e, t], m[:, e, c0:c0 + n], k == 0, k == 2 * 3 - 1)
                        k += 1
                return i

            def max_t(b, negm, mx, mtr):
                wait(pe, mx, 16 * b + H)
                for t in range(2):
                    i = nc.tensor.transpose(ps[2][0:H, t * P:(t + 1) * P], negm[:, t, :], idf[:, :])
                i.then_inc(mtr, 1)

            def project_heads(b, ov_, fa, on_, fb, of_, wo, od):
                def to_tokens():
                    wait(pe, ov_, NG * b + NG)
                    for tt in range(2):
                        for g in range(NG):
                            i = nc.tensor.transpose(ps[6 + tt][:, g * P:(g + 1) * P],
                                                    ov[:, g, tt * P:(tt + 1) * P], idf[:, :])
                    i.then_inc(fa, 1)

                def back():
                    wait(pe, on_, b + 1)
                    for e in range(ET):
                        for tt in range(2):
                            a = otk[:, tt, :, :].rearrange("p h c -> p (h c)")[:, e * P:(e + 1) * P]
                            i = nc.tensor.transpose(ps[6][:, (2 * e + tt) * P:(2 * e + tt + 1) * P], a, idf[:, :])
                    i.then_inc(fb, 1)

                def project():
                    wait(pe, of_, b + 1)
                    for tt in range(2):
                        for e in range(ET):
                            i = mm(ps[7][:, tt * E:(tt + 1) * E], otf[:, e, tt * P:(tt + 1) * P], wo[:, e, :],
                                   e == 0, e == ET - 1)
                    i.then_inc(od, 1)
                return to_tokens, back, project

            def close1(b):
                return project_heads(b, ov1, fa1, on1, fb1, of1, wo1, o1)

            def close2(b):
                return project_heads(b, ov2, fa2, on2, fb2, of2, wo2, o2)

            def transpose_x(b):
                wait(pe, t2e, 8 * b)
                wait(pe, xbd, b + 1)
                for e in range(ET):
                    for tt in range(2):
                        i = nc.tensor.transpose(ps[0][:, (2 * e + tt) * P:(2 * e + tt + 1) * P],
                                                xb[:, tt, e * P:(e + 1) * P], idf[:, :])
                i.then_inc(tr0, 1)

            def stage_p1(b, after):
                wait(pe, v2d, b)
                wait(pe, xtld, b + 1)

                def step_proj(i):
                    tt, c = i // 9, i % 9
                    if i >= 2:
                        j = i - 2
                        if j % 9 == 8:
                            wait(pe, v1d, 2 * b + j // 9 + 1)
                        else:
                            wait(pe, roped, 16 * b + 8 * (j // 9) + j % 9 + 1)
                    if c < 8:
                        c0 = (QC, KC)[c % 2] + (c // 2) * CH
                        proj(ps[i % 2][:, 0:CH], c0, CH, tt).then_inc(p1d, 1)
                    else:
                        proj(ps[i % 2][:, 0:H * D], VC, H * D, tt).then_inc(p1d, 1)

                def step_tr(i, n):
                    wait(pe, tokd, 16 * b + n + 1)
                    if n == 0:
                        wait(pe, mte2, b)
                    if n >= 2:
                        wait(pe, qke, 16 * b + n - 1)
                    for j in range(G):
                        t = nc.tensor.transpose(ps[2 + n % 2][:, j * P:(j + 1) * P], tok[:, n % 4, j, :],
                                                idf[:, :])
                    t.then_inc(tr1, 1)

                order(step_proj, step_tr, after)

            def project_qk2(b, tt):
                if tt == 0:
                    wait(pe, roped, 16 * b + 16)
                else:
                    wait(pe, s2d, 4 * b + 2)
                proj(ps[0][:, :], Q2C, 2 * H * D, tt).then_inc(p2d, 1)

            def project_v2(b):
                wait(pe, v1d, 2 * b + 2)
                proj(ps[1][:, 0:H * D], V2C, H * D, 0)
                proj(ps[1][:, H * D:2 * H * D], V2C, H * D, 1).then_inc(p2d, 1)

            def stage_p2(b, after):
                max_t(b, negm1, mx1, mtr1)
                for u in range(8):
                    if u == 1:
                        wait(pe, mte1, b + 1)
                    if u % 2 == 0 and u < 4:
                        wait(pe, s2d, 4 * b + u + 2)
                    if u >= 3:
                        wait(pe, t2e, 8 * b + u - 2)
                        if (u - 3) % 2 == 0:
                            wait(pe, t2o, 4 * b + (u - 3) // 2 + 1)
                    a = (qs, ks)[u % 2][:, u // 4, :, :].rearrange("p h c -> p (h c)").bitcast(F32)
                    for j in range(4):
                        p0 = (4 * (u // 2 % 2) + j) * P
                        i = nc.tensor.transpose(bank2(u)[:, j * P:(j + 1) * P], a[:, p0:p0 + P], idf[:, :])
                    i.then_inc(tr2, 1)
                    after.get(u, lambda: None)()

            def raw_scores(o, q, k):
                for t in range(2):
                    mm(o[:, 3 * P * t:3 * P * t + P], idb[:, :], maskb[:, 0, :], t == 0, False)
                for t in range(2):
                    i = mm(o[:, t * S:(t + 1) * S], q[:, t * P:(t + 1) * P], k, False, t == 1)
                return i

            def max1(b):
                def head(h):
                    if h == 0:
                        wait(pe, qke, 16 * b + 16)
                    if h % 2 == 0:
                        wait(pe, rrd, H // 2 * b + h // 2 + 1)
                        wait(pe, rkd, H // 2 * b + h // 2 + 1)
                    if h >= 2:
                        wait(pe, mx1, 16 * b + h - 1)
                    j = (h // 2 % 2, h % 2)
                    raw_scores(ps[2 + h % 2], qr[:, j[0], j[1], :], kr[:, j[0], j[1], :]).then_inc(m1d, 1)
                return head

            def max2(b):
                def head(h):
                    if h == 0:
                        wait(pe, t2e, 8 * b + 8)
                        wait(pe, t2o, 4 * b + 4)
                    if h >= 2:
                        wait(pe, mx2, 16 * b + h - 1)
                    raw_scores(ps[2 + h % 2], qt2[:, h, :], kt2[:, h // 2, :]).then_inc(m2d, 1)
                return head

            def heads(b, scores_t, st, ex_, exm, pv, ov_, v, before_h0, before_pv0, max_head, after):
                before_h0()

                def values(g):
                    wait(pe, exm, 16 * b + G * (g + 1))
                    if g == 0:
                        before_pv0()
                    if g >= 2:
                        wait(pe, ov_, NG * b + g - 1)
                    for k, (o0, e0, n) in enumerate(((0, P, S), (P, 0, P))):
                        for j in range(G):
                            h = G * g + j
                            i = mm(ps[6 + g % 2][PADV * j:PADV * (j + 1), o0:o0 + n], v[:, k, h, :],
                                   ex[:, h % (2 * G), e0:e0 + n], k == 0, k == 1, tile_position=(0, PADV * j))
                    i.then_inc(pv, 1)

                for h in range(H):
                    if h >= 2:
                        wait(pe, ex_, 16 * b + h - 1)
                    scores_t(h, ps[4 + h % 2]).then_inc(st, 1)
                    if h > 0:
                        max_head(h - 1)
                    if h >= G and h % G == G - 1:
                        values(h // G - 1)
                    after.get(h, lambda: None)()
                max_head(H - 1)
                return lambda: values(NG - 1)

            def scores1(h, o):
                mm(o[:, P:2 * P], kt[:, h, P:S], qt[:, h, P:S], True, True)
                return mm(o[:, 2 * P:4 * P], kt[:, h, 0:P], qt[:, h, :], True, True)

            def scores2(h, o):
                mm(o[:, 0:2 * P], kt2[:, h // 2, P:S], qt2[:, h, :], True, False)
                mm(o[:, 2 * P:4 * P], kt2[:, h // 2, 0:P], qt2[:, h, :], False, False)
                mm(o[:, P:2 * P], idb[:, :], maskb[:, 1, :], False, True)
                return mm(o[:, 2 * P:3 * P], idb[:, :], maskb[:, 1, :], False, True)

            def stage_t1(b, after):
                def before_h0():
                    wait(pe, ex2, 16 * b)
                    wait(pe, md1, 16 * b + 16)
                    wait(pe, v1d, 2 * b + 2)
                return heads(b, scores1, st1, ex1, exm1, pv1, ov1, v1, before_h0, lambda: wait(pe, x2d, b), max2(b), after)

            def stage_t2(b, max_head, after):
                def before_h0():
                    wait(pe, ex1, 16 * b + 16)
                    wait(pe, md2, 32 * b + 32)
                    wait(pe, v2d, b + 1)
                heads(b, scores2, st2, ex2, ex2, pv2, ov2, v2, before_h0, lambda: wait(pe, sd, b + 1), max_head,
                      after)()


            def next_mha(b):
                return {5: lambda: project_v2(b), 10: lambda: project_qk2(b, 1)}

            def batch(b, first, more):
                after2, after1 = {}, {}
                if not first:
                    to_tokens, back, project = close2(b - 1)
                    after2 = {0: to_tokens}
                    after1 = {0: back, 3: project}
                stage_p2(b, after2)
                if more:
                    after1[10] = lambda: transpose_x(b + 1)
                last_values = stage_t1(b, after1)
                if more:
                    to_tokens, back, project = close1(b)

                    def after_first():
                        last_values()
                        max_t(b, negm2, mx2, mtr2)
                    stage_p1(b + 1, {0: after_first, 1: to_tokens, 4: back, 7: project,
                                     17: lambda: project_qk2(b + 1, 0)})
                    stage_t2(b, max1(b + 1), next_mha(b + 1))
                else:
                    last_values()
                    max_t(b, negm2, mx2, mtr2)
                    closing = dict(zip((0, 3, 5), close1(b)))

                    def between(h):
                        if h < EARLY:
                            route_transpose(h)
                        if 1 <= h <= EARLY:
                            route_logits(h - 1)
                        closing.get(h, lambda: None)()
                    between(0)
                    stage_t2(b, lambda h: None, {h: lambda h=h: between(h + 1) for h in range(H - 1)})

            def route_bank(t):
                return ps[t % 4] if t < EARLY else ps[6 + t % 2]

            def route_transpose(t):
                wait(pe, xb2d, t + 1)
                if t == 0:
                    wait(pe, mte2, B)
                    wait(pe, t2e, 8 * B)
                    wait(pe, v2d, B)
                if t < EARLY:
                    wait(pe, lgk, t - 3)
                for e in range(ET):
                    i = nc.tensor.transpose(route_bank(t)[:, e * P:(e + 1) * P], xb2[:, t % 2, e * P:(e + 1) * P],
                                            idf[:, :])
                i.then_inc(tr3, 1)

            def route_logits(t):
                wait(pe, ytd, t + 1)
                for e in range(ET):
                    i = mm(route_bank(t)[:, E:E + NE], yt[:, t % 2, e, :], wr[:, e, :], e == 0, e == ET - 1)
                i.then_inc(lgd, 1)

            pe.wait_ge(s_lr, 16 * 4)
            w = 0
            for m in range(ET):
                cols = slice(m * P, (m + 1) * P)
                if m == 1:
                    pe.wait_ge(s_k, 16 * 6)
                    transpose_x(0)
                for c in range(NG + 1):
                    if w >= 7:
                        pe.wait_ge(combl, w - 6)
                    if c < NG:
                        o = ps[1 + w % 7][:, 0:CH]
                        for a in range(2):
                            i = mm(o, w_dq_raw[0:RT, a, cols], w_uqr_raw[0:RT, a, c * CH:(c + 1) * CH], a == 0, a == 1)
                    else:
                        i = mm(ps[1 + w % 7][:, :], w_dkv_raw[:, cols], w_ukv_raw[:, :], True, True)
                    i.then_inc(comb, 1)
                    w += 1

            pe.wait_ge(clear, 2)
            pe.wait_ge(combl, N_COMB)
            pe.wait_ge(wdone, 1)
            pe.wait_ge(wdonep, 1)
            stage_p1(0, {17: lambda: project_qk2(0, 0)})
            pe.wait_ge(s_c, 16 * 4)
            pe.wait_ge(cast, 2)
            for h in range(H):
                max1(0)(h)
                next_mha(0).get(h, lambda: None)()
            batch(0, True, True)
            with pe.Fori(1, last) as b:
                batch(b, False, True)
            batch(last, False, False)

            def gate_up(e, s, c, it):
                n = 16 * e + 4 * c + it
                pe.wait_ge(weld, e + 1)
                for w0, bank, done, free in ((WG, 0, gd, sgd), (WU, 2, ud, hfd)):
                    wait(pe, free, n - 1)
                    k = 0
                    for wt, xt in ((weh, x2h), (wel, x2h), (weh, x2l)):
                        for m in range(ET):
                            a = wt[:, s, w0 + m * FF + it * P:w0 + m * FF + (it + 1) * P]
                            i = mm(ps[bank + it % 2][:, :], a, xt[:, m, bass.ds(c * TC, TC)], k == 0, k == 5)
                            k += 1
                    i.then_inc(done, 1)

            def down(e, s, c, it):
                n = 16 * e + 4 * c + it
                pe.wait_ge(hld, n + 1)
                if it == 0:
                    wait(pe, yd, 4 * e + c)
                for t in range(TC // P):
                    o = ps[4 + t // 2][:, (t % 2) * E:(t % 2 + 1) * E]
                    for k, (a, m) in enumerate(((hh, weh), (hh, wel), (hl, weh))):
                        i = mm(o, a[:, it % 2, t * P:(t + 1) * P], m[:, s, WD + it * E:WD + (it + 1) * E],
                               it == 0 and k == 0 and t % 2 == 0, it == IT - 1 and k == 2)
                i.then_inc(dd, 1)

            def expert(e, s, first, final):
                def chunk(c, nxt, after):
                    for it in range(1, IT):
                        gate_up(e, s, c, it)
                        down(e, s, c, it - 1)
                        after.get(it, lambda: None)()
                    nxt()
                    down(e, s, c, IT - 1)
                if first:
                    def last_transposes():
                        for t in range(EARLY, TT):
                            route_transpose(t)

                    def last_logits():
                        for t in range(EARLY, TT):
                            route_logits(t)
                    chunk(0, lambda: gate_up(e, s, 1, 0), {2: last_transposes, 3: last_logits})
                    pe.wait_ge(x2ld, TT)
                with pe.Fori(1 if first else 0, NC - 1) as c:
                    chunk(c, lambda: gate_up(e, s, c + 1, 0), {})
                chunk(NC - 1, (lambda: None) if final else (lambda: gate_up(e + 1, 1 - s, 0, 0)), {})

            to_tokens, back, project = close2(last)
            to_tokens()
            pe.wait_ge(x2ld, EARLY)
            pe.wait_ge(lgk, EARLY)
            gate_up(0, 0, 0, 0)
            back()
            project()
            expert(0, 0, True, False)
            expert(1, 1, False, False)
            with pe.Fori(1, NE // 2 - 1) as i:
                for s in range(2):
                    expert(2 * i + s, s, False, False)
            expert(NE - 2, 0, False, False)
            expert(NE - 1, 1, False, True)

        @block.scalar
        def _(act):
            def copy(o, a):
                return nc.scalar.activation(o, a, ACT.Copy)

            for dst, src in ((idf[:, :], ident), (mask_f[:, 0, :], mask), (mask_f[:, 1, :], mask_t),
                             (seen[:, 0, :], seen_t), (cos_t[:, :, :], cosines), (sin_t[:, :, :], sines)):
                act.dma_start(dst, src).then_inc(s_k, 16)

            def products_high(m):
                for c in range(NG + 1):
                    w = (NG + 1) * m + c
                    act.wait_ge(comb, w + 1)
                    o = ps[1 + w % 7]
                    if c < NG:
                        copy(wh[:, m, QC + c * CH:QC + (c + 1) * CH], o[:, 0:CH]).then_inc(combh, 1)
                    else:
                        copy(wh[:, m, KC:VC].rearrange("p (h c) -> p h c", h=H)[:, :, RD:HW],
                             o[:, 0:H * D].rearrange("p (h c) -> p h c", h=H))
                        copy(wh[:, m, VC:VC + H * D], o[:, H * D:2 * H * D]).then_inc(combh, 1)

            def x_high(b):
                wait(act, tr0, b + 1)
                wait(act, p2d, 3 * b)
                copy(xth[:, :, :].rearrange("p e t -> p (e t)"), ps[0][:, :]).then_inc(xthd, 1)

            products_high(0)
            x_high(0)
            act.wait_ge(s_w, 16 * 2)
            for m in range(ET):
                copy(rope_part(wh, m), w_cols_raw[:, m, 0:H * RD].rearrange("p (h c) -> p h c", h=H)).then_inc(wfh, 1)
            products_high(1)
            for m in range(ET):
                nc.scalar.activation(wh[:, m, Q2C:WC], w_cols_raw[:, m, H * RD:], ACT.Copy,
                                     scale=ln1[:, m:m + 1]).then_inc(wfh, 1)
            act.wait_ge(s_k, 16 * 6)
            copy(idb[:, :], idf[:, :]).then_inc(cast, 1)
            copy(maskb[:, :, :], mask_f[:, :, :]).then_inc(cast, 1)

            def max_t1(b):
                wait(act, mtr1, b + 1)
                wait(act, md2, 32 * b)
                copy(mt[:, :].bitcast(F32), ps[2][0:H, 0:S]).then_inc(mte1, 1)

            def max_t2(b):
                wait(act, mtr2, b + 1)
                wait(act, md1, 16 * b + 16)
                copy(mt[:, :], ps[2][0:H, 0:S]).then_inc(mte2, 1)

            def keep_back(b, fb, of_, od):
                wait(act, fb, b + 1)
                copy(otf[:, :, :].rearrange("p e t -> p (e t)"), ps[6][:, :]).then_inc(of_, 1)

            def rounded(b, g):
                wait(act, qke, 16 * b + 10 + 2 * (g // 2))
                wait(act, m1d, 16 * b + 2 * max(g - 1, 0))
                copy(kr[:, g % 2, :, :], kt[:, 2 * g:2 * g + 2, :]).then_inc(rkd, 1)

            def stage_p1(b, after):
                if not isinstance(b, int) or b > 0:
                    max_t2(b - 1)
                wait(act, st1, 16 * b)
                wait(act, pv1, NG * b)

                def step_proj(i):
                    if i % 9 == 8:
                        wait(act, p1d, 18 * b + i + 1)
                        copy(v1[:, i // 9, :, 0:D],
                             ps[i % 2][:, 0:H * D].rearrange("p (h c) -> p h c", h=H)).then_inc(v1d, 1)

                def step_tr(i, n):
                    wait(act, tr1, 16 * b + n + 1)
                    g, tt = n % 8 // 2, n // 8
                    copy((qt, kt)[n % 2][:, G * g:G * (g + 1), tt * P:(tt + 1) * P],
                         ps[2 + n % 2][:, :].rearrange("p (h t) -> p h t", h=G)).then_inc(qke, 1)

                order(step_proj, step_tr, after)

            def qk2_high(b, tt):
                wait(act, rbd, b + 1)
                wait(act, p2d, 3 * b + 1 + 2 * tt)
                for a, o in enumerate((qs, ks)):
                    nc.scalar.activation(o[:, tt, :, 0:D],
                                         ps[0][:, a * H * D:(a + 1) * H * D].rearrange("p (h c) -> p h c", h=H),
                                         ACT.Copy, scale=rb[:, tt:tt + 1]).then_inc(hi2, 1)

            def keep_v2(b):
                wait(act, p2d, 3 * b + 2)
                wait(act, pv2, NG * b)
                for tt in range(2):
                    i = nc.scalar.activation(v2[:, tt, :, 0:D],
                                             ps[1][:, tt * H * D:(tt + 1) * H * D].rearrange("p (h c) -> p h c", h=H),
                                             ACT.Copy, scale=rb[:, tt:tt + 1])
                i.then_inc(v2d, 1)

            def stage_p2(b, after):
                max_t1(b)
                wait(act, st2, 16 * b)
                for u in range(8):
                    wait(act, tr2, 8 * b + u + 1)
                    t = slice(u // 4 * P, (u // 4 + 1) * P)
                    a = bank2(u)[:, :].rearrange("p (h t) -> p h t", h=4)
                    if u % 2 == 0:
                        h0 = 8 * (u // 2 % 2)
                        copy(qt2[0:ST, h0:h0 + 8:2, t], a[0:ST, :, :]).then_inc(t2e, 1)
                    else:
                        copy(kt2[:, 4 * (u // 2 % 2):4 * (u // 2 % 2) + 4, t], a).then_inc(t2e, 1)
                    after.get(u, lambda: None)()

            def exps(b, st, ex_, pv, ov_, pv_before, fa_before, scale, after):
                pv_before()

                def keep(g):
                    if g == 0:
                        fa_before()
                    wait(act, pv, NG * b + g + 1)
                    copy(ov[:, g, :], ps[6 + g % 2][:, 0:S]).then_inc(ov_, 1)

                for h in range(H):
                    g = h // G
                    wait(act, st, 16 * b + h + 1)
                    if h % G == 0 and g >= 2:
                        wait(act, pv, NG * b + g - 1)
                    nc.scalar.activation(ex[:, h % (2 * G), :], ps[4 + h % 2][:, P:4 * P], ACT.Exp,
                                         scale=scale).then_inc(ex_, 1)
                    if h in (9, 13):
                        keep((h - 9) // G)
                    after.get(h, lambda: None)()
                keep(2)
                keep(3)

            act.wait_ge(clear, 2)

            def batch(b, first, more):
                stage_p2(b, {})
                after = {1: lambda: keep_v2(b)}
                if not first:
                    after[0] = lambda: keep_back(b - 1, fb2, of2, o2)
                if more:
                    after[11] = lambda: x_high(b + 1)
                exps(b, st1, ex1, pv1, ov1, lambda: wait(act, pv2, NG * b), lambda: wait(act, fa2, b),
                     float(HW) ** -0.5, after)
                if more:
                    stage_p1(b + 1, {4: lambda: keep_back(b, fb1, of1, o1), 14: lambda: rounded(b + 1, 0),
                                     16: lambda: rounded(b + 1, 1)})
                    after = {h: lambda h=h: rounded(b + 1, h // 2 + 1) for h in range(2, H - 2, 2)}
                    after[1] = lambda: qk2_high(b + 1, 0)
                    after[11] = lambda: qk2_high(b + 1, 1)
                else:
                    max_t2(b)
                    after = {h: lambda h=h: scaled(h + 1) for h in range(EARLY - 1)}

                    def scaled3():
                        scaled(3)
                        keep_back(b, fb1, of1, o1)
                    after[2] = scaled3
                    scaled(0)
                exps(b, st2, ex2, pv2, ov2, lambda: wait(act, pv1, NG * b + NG), lambda: wait(act, fa1, b + 1),
                     float(D) ** -0.5, after)
                if not more:
                    keep_back(b, fb2, of2, o2)

            def scaled(t):
                wait(act, tr3, t + 1)
                wait(act, lgd, t - 1)
                wait(act, x2ld, t - 1)
                o = ps[t % 4] if t < EARLY else ps[6 + t % 2]
                for e in range(ET):
                    a = nc.scalar.activation(yt[:, t % 2, e, :], o[:, e * P:(e + 1) * P], ACT.Copy,
                                             scale=ln2[:, e:e + 1])
                a.then_inc(ytd, 1)

            act.wait_ge(wdonep, 1)
            act.wait_ge(cast, 2)
            act.wait_ge(wdone, N_DIRECT)
            stage_p1(0, {14: lambda: rounded(0, 0), 16: lambda: rounded(0, 1)})
            for g in range(2, H // 2):
                rounded(0, g)
                if g == 2:
                    qk2_high(0, 0)
                if g == 6:
                    qk2_high(0, 1)
            batch(0, True, True)
            with act.Fori(1, last) as b:
                batch(b, False, True)
            batch(last, False, False)

            def silu(n, it):
                wait(act, gd, 4 * n + it + 1)
                wait(act, hfd, 4 * n + it - 1)
                nc.scalar.activation(sg[:, it % 2, :], ps[it % 2][:, :], ACT.Silu).then_inc(sgd, 1)

            def silus(n):
                for it in range(IT):
                    silu(n, it)

            for it in range(3):
                silu(0, it)
            for t in range(EARLY, TT):
                scaled(t)
            silu(0, 3)
            act.wait_ge(gch, 1)
            nc.scalar.activation(gate[:, 1, :], gate[:, 0, :], ACT.Exp).then_inc(gex, 1)
            silus(1)
            with act.Fori(2, NE * NC - NC + 1) as n:
                silus(n)

            def ffn_silu(j):
                act.wait_ge(yd, NE * NC - NC + j + 1)
                wait(act, mud, j)
                if j < NC - 1:
                    nc.scalar.activation(gl[:, :, :], xn[:, 4 * j:4 * j + 4, :], ACT.Silu).then_inc(gld, 1)
                else:
                    for k in range(2):
                        nc.scalar.activation(gl[:, 2 * k:2 * k + 2, :], xn[:, 4 * j + 2 * k:4 * j + 2 * k + 2, :],
                                             ACT.Silu).then_inc(gld, 1)

            for c in range(1, NC):
                for it in range(IT):
                    silu(NE * NC - NC + c, it)
                    if it == 2:
                        ffn_silu(c - 1)
            ffn_silu(NC - 1)

        @block.vector
        def _(dve):
            def copy(o, a):
                return nc.vector.tensor_copy(o, a)

            def minus(o, a, b):
                return nc.vector.tensor_tensor(o, a, b.bitcast(F32), ALU.subtract)

            def norm_stats(t):
                for i in range(t.start, t.stop):
                    nc.vector.bn_stats(stats[:, i, :], xn[:, i, :]).then_inc(st_a, 1)

            def variances(t, n):
                dve.wait_ge(st_a, t.stop)
                for i in range(t.start, t.stop):
                    nc.vector.bn_aggr(mv[:, i, :], stats[:, i, :]).then_inc(st_b, 1)
                dve.wait_ge(st_b, t.stop + n)
                nc.vector.tensor_scalar(msq[:, t], mv[:, t, 1], EPS, None, ALU.add).then_inc(st_b, 1)

            dve.wait_ge(s_x[0], 16)
            norm_stats(LOADED[0])
            variances(LOADED[0], 0)
            dve.wait_ge(s_x[1], 16)
            norm_stats(LOADED[1])

            def products_low(m):
                for c in range(NG + 1):
                    w = (NG + 1) * m + c
                    dve.wait_ge(combh, w + 1)
                    o = ps[1 + w % 7]
                    if c < NG:
                        cs = slice(QC + c * CH, QC + (c + 1) * CH)
                        minus(wl[:, m, cs], o[:, 0:CH], wh[:, m, cs]).then_inc(combl, 1)
                    else:
                        kh, kl = (a[:, m, KC:VC].rearrange("p (h c) -> p h c", h=H)[:, :, RD:HW] for a in (wh, wl))
                        minus(kl, o[:, 0:H * D].rearrange("p (h c) -> p h c", h=H), kh)
                        cs = slice(VC, VC + H * D)
                        minus(wl[:, m, cs], o[:, H * D:2 * H * D], wh[:, m, cs]).then_inc(combl, 1)

            def copy_batch(b):
                wait(dve, tr0, b)
                copy(xb[:, :, :], xn[:, bass.ds(2 * b, 2), :]).then_inc(xbd, 1)

            def x_low(b):
                wait(dve, xthd, b + 1)
                minus(xtl[:, :, :].rearrange("p e t -> p (e t)"), ps[0][:, :],
                      xth[:, :, :].rearrange("p e t -> p (e t)")).then_inc(xtld, 1)

            dve.wait_ge(powd, 1)
            for t in range(2):
                normalised(t).then_inc(xnd, 1)
            dve.wait_ge(xnd, 2)
            copy_batch(0)
            products_low(0)
            x_low(0)
            dve.wait_ge(s_x[2], 16)
            norm_stats(LOADED[2])
            products_low(1)
            dve.wait_ge(wfh, 2)
            minus(rope_part(wl, 1), w_cols_raw[:, 1, 0:H * RD].rearrange("p (h c) -> p h c", h=H),
                  rope_part(wh, 1)).then_inc(wdone, 1)
            variances(slice(2, TT), 1)

            def mha_weights_low(m):
                dve.wait_ge(wfh, ET + m + 1)
                nc.vector.scalar_tensor_tensor(out=wl[:, m, Q2C:WC], in0=w_cols_raw[:, m, H * RD:],
                                               scalar=ln1[:, m:m + 1], in1=wh[:, m, Q2C:WC].bitcast(F32),
                                               op0=ALU.mult, op1=ALU.subtract).then_inc(wdone, 1)

            def copy_rms1(b):
                wait(dve, v2d, b)
                copy(rb[:, :], rms1[:, bass.ds(2 * b, 2)]).then_inc(rbd, 1)

            def close_heads(b, fa, rc, on_, od, keep):
                def normalise():
                    wait(dve, fa, b + 1)
                    for tt in range(2):
                        a = ps[6 + tt][:, :].rearrange("p (h c) -> p h c", h=H)
                        i = nc.vector.reciprocal(rec[:, tt, :], a[:, :, V1])
                    i.then_inc(rc, 1)
                    wait(dve, rc, b + 1)
                    for tt in range(2):
                        a = ps[6 + tt][:, :].rearrange("p (h c) -> p h c", h=H)
                        i = nc.vector.tensor_tensor(otk[:, tt, :, :], a[:, :, 0:D],
                                                    rec[:, tt, :].unsqueeze(2).broadcast_to([P, H, D]), ALU.mult)
                    i.then_inc(on_, 1)

                def kept():
                    wait(dve, od, b + 1)
                    keep(b)
                return normalise, kept

            def keep_s(b):
                wait(dve, sst, 16 * b)
                copy(s_b[:, :, :].rearrange("p t e -> p (t e)"), ps[7][:, :]).then_inc(sd, 1)

            def keep_x2(b):
                a = xn[:, bass.ds(2 * b, 2), :]
                nc.vector.tensor_tensor(a, ps[7][:, :].rearrange("p (t e) -> p t e", t=2), a, ALU.add).then_inc(x2d, 1)

            def close1(b):
                return close_heads(b, fa1, rc1, on1, o1, keep_s)

            def close2(b):
                return close_heads(b, fa2, rc2, on2, o2, keep_x2)

            def stage_p1(b, after):
                for n in range(16):
                    tt = n // 8
                    i = 9 * tt + n % 8
                    wait(dve, p1d, 18 * b + i + 1)
                    wait(dve, tr1, 16 * b + max(n - 3, 0))
                    wait(dve, tokd, 16 * b + max(n - 1, 0))
                    a = ps[i % 2][:, 0:CH].rearrange("p (h c) -> p h c", h=G)
                    nc.vector.tensor_tensor(tok[:, n % 4, :, 0:HW], a,
                                            cos_t[:, tt:tt + 1, :].broadcast_to([P, G, HW]), ALU.mult)
                    sw = a[:, :, 0:RD].rearrange("p h (s d) -> p h s d", s=2)[:, :, ::-1, :]
                    sn = sin_t[:, tt:tt + 1, :].broadcast_to([P, G, RD]).rearrange("p h (s d) -> p h s d", s=2)
                    nc.vector.tensor_tensor(swp[:, n % 2, :, :].rearrange("p h (s d) -> p h s d", s=2), sw, sn,
                                            ALU.mult).then_inc(roped, 1)
                    after.get(n, lambda: None)()

            def rounded(b, g):
                wait(dve, qke, 16 * b + 9 + 2 * (g // 2))
                wait(dve, m1d, 16 * b + 2 * max(g - 1, 0))
                copy(qr[:, g % 2, :, :], qt[:, 2 * g:2 * g + 2, :]).then_inc(rrd, 1)

            def stage_m1(b, after):
                wait(dve, mtr1, b)
                for h in range(H):
                    if h % 2 == 0 and 2 <= h < H - 2:
                        rounded(b, h // 2 + 1)
                    maxima(b, h, h, negm1, m1d, mx1)
                    after.get(h, lambda: None)()

            def splits(b):
                def both(a):
                    again2(b, 1, a)
                    low2(b, 1, a)
                return {3: lambda: (again2(b, 0, 0), again2(b, 0, 1)), 5: lambda: low2(b, 0, 0),
                        7: lambda: low2(b, 0, 1), 12: lambda: both(0), 14: lambda: both(1)}

            def causal(b, h):
                wait(dve, ex1, 16 * b + h + 1)
                a = ex[:, h % (2 * G), 0:2 * P].rearrange("p (a q) -> p a q", a=2)
                nc.vector.tensor_tensor(a, a, seen[:, 0:1, :].broadcast_to([P, 2, P]), ALU.min).then_inc(exm1, 1)

            def stage_m2(b, after):
                wait(dve, mtr2, b)
                for h in range(H):
                    causal(b, h)
                    maxima(b, h, (h % 2) * (H // 2) + h // 2, negm2, m2d, mx2)
                    after.get(h, lambda: None)()

            def maxima(b, h, col, negm, md, mx):
                wait(dve, md, 16 * b + h + 1)
                o = ps[2 + h % 2]
                nc.vector.tensor_reduce(negm[:, 0, col:col + 1], o[:, 0:P], AX.X, ALU.max, negate=True)
                nc.vector.tensor_reduce(negm[:, 1, col:col + 1], o[:, S:2 * S], AX.X, ALU.max,
                                        negate=True).then_inc(mx, 1)

            def again2(b, tt, a):
                wait(dve, hi2, 4 * b + 2 * tt + 2)
                o = (qs, ks)[a][:, tt, :, :]
                copy(o[:, :, (1 + a) * D:(2 + a) * D], o[:, :, 0:D])

            def low2(b, tt, a):
                o = (qs, ks)[a][:, tt, :, :]
                nc.vector.scalar_tensor_tensor(
                    out=o[:, :, (2 - a) * D:(3 - a) * D],
                    in0=ps[0][:, a * H * D:(a + 1) * H * D].rearrange("p (h c) -> p h c", h=H),
                    scalar=rb[:, tt:tt + 1], in1=o[:, :, 0:D].bitcast(F32),
                    op0=ALU.mult, op1=ALU.subtract).then_inc(s2d, 1)

            def odd_heads(b, i):
                wait(dve, tr2, 8 * b + 2 * i + 1)
                t = slice(i // 2 * P, (i // 2 + 1) * P)
                h0 = 8 * (i % 2)
                copy(qt2[ST:P, h0 + 1:h0 + 8:2, t],
                     bank2(2 * i)[ST:P, :].rearrange("p (h t) -> p h t", h=4)).then_inc(t2o, 1)

            def batch(b, first, more):
                normalise, kept = ((lambda: None),) * 2 if first else close2(b - 1)
                wait(dve, st2, 16 * b)
                odd_heads(b, 0)
                odd_heads(b, 1)
                odd_heads(b, 2)
                normalise()
                odd_heads(b, 3)
                after = {4: kept}
                if not first:
                    after[6] = lambda: stats_x2(b - 1)
                if not more:
                    after[8] = lambda: mean_squares2(0)
                if more:
                    after[7] = lambda: copy_batch(b + 1)
                    after[8] = lambda: copy_rms1(b + 1)
                    after[12] = lambda: x_low(b + 1)
                stage_m2(b, after)
                if more:
                    normalise, kept = close1(b)
                    stage_p1(b + 1, {1: normalise, 7: kept, 12: lambda: rounded(b + 1, 0),
                                     14: lambda: rounded(b + 1, 1)})
                    stage_m1(b + 1, splits(b + 1))
                else:
                    dve.wait_ge(pv1, NG * B)
                    normalise, kept = close1(b)
                    scale_tokens(0)
                    scale_tokens(1)
                    normalise()
                    for t in range(EARLY):
                        keep_columns(t)
                        keep_logits(t)
                        if t + 2 < EARLY:
                            scale_tokens(t + 2)
                        if t == 4:
                            kept()
                        if t >= EARLY - 1 - PIECES and t < EARLY - 1:
                            piece_high(0, 0, t - (EARLY - 1 - PIECES))

            PIECES = 4

            def piece_high(e, s, k):
                cs = slice(k * WE // PIECES, (k + 1) * WE // PIECES)
                if k == 0:
                    wait(dve, rawd[s], 8 * e + 16 - 8 * s)
                    wait(dve, dd, 16 * (e - 1))
                copy(weh[:, s, cs], raw[:, s, cs]).then_inc(wehd, 1)

            def piece_low(e, s, k):
                cs = slice(k * WE // PIECES, (k + 1) * WE // PIECES)
                wait(dve, wehd, PIECES * e + k + 1)
                i = minus(wel[:, s, cs], raw[:, s, cs], weh[:, s, cs])
                if k == PIECES - 1:
                    i.then_inc(weld, 1)

            def split_piece(e, s, k):
                piece_high(e, s, k)
                piece_low(e, s, k)

            def stats_x2(b):
                dve.wait_ge(x2d, b + 1)
                for t in range(2):
                    nc.vector.bn_stats(stats[:, bass.ds(2 * b + t, 1), :].rearrange("p o c -> p (o c)"),
                                       xn[:, bass.ds(2 * b + t, 1), :].rearrange("p o e -> p (o e)")).then_inc(st_c, 1)

            def mean_squares2(k):
                t = ROUTED[k]
                dve.wait_ge(st_c, t.stop)
                for i in range(t.start, t.stop):
                    nc.vector.bn_aggr(mv[:, i, :], stats[:, i, :]).then_inc(st_d, 1)
                dve.wait_ge(st_d, t.stop)
                nc.vector.tensor_tensor(msq[:, t], mv[:, t, 0], mv[:, t, 0], ALU.mult).then_inc(ms2, 1)
                dve.wait_ge(ms2, 2 * k + 1)
                nc.vector.scalar_tensor_tensor(out=msq[:, t], in0=msq[:, t], scalar=EPS, in1=mv[:, t, 1],
                                               op0=ALU.add, op1=ALU.add).then_inc(ms2, 1)

            def scale_tokens(t):
                wait(dve, rm2, 1 if t < EARLY else 2)
                wait(dve, tr3, t - 1)
                nc.vector.tensor_scalar(xb2[:, t % 2, :], xn[:, t, :], rstd[:, t:t + 1], None,
                                        ALU.mult).then_inc(xb2d, 1)

            def keep_columns(t):
                wait(dve, ytd, t + 1)
                cs = slice(t * P, (t + 1) * P)
                copy(x2h[:, :, cs], yt[:, t % 2, :, :]).then_inc(x2hd, 1)
                wait(dve, x2hd, t + 1)
                minus(x2l[:, :, cs], yt[:, t % 2, :, :], x2h[:, :, cs]).then_inc(x2ld, 1)

            def keep_logits(t):
                wait(dve, lgd, t + 1)
                o = ps[t % 4] if t < EARLY else ps[6 + t % 2]
                copy(lg[:, t, :], o[:, E:E + NE]).then_inc(lgk, 1)

            dve.wait_ge(s_k, 16 * 6)
            dve.wait_ge(clear, 2)

            def mean_squares():
                dve.wait_ge(powd, 2)
                nc.vector.tensor_tensor(msq[:, :], mv[:, :, 1], rstd[:, :], ALU.mult).then_inc(msd, 1)
                dve.wait_ge(msd, 1)
                nc.vector.tensor_tensor(msq[:, :], msq[:, :], rstd[:, :], ALU.mult).then_inc(msd, 1)
                dve.wait_ge(msd, 2)
                nc.vector.tensor_scalar(msq[:, :], msq[:, :], EPS, None, ALU.add).then_inc(msd, 1)

            later = {n: lambda n=n: normalised(n).then_inc(xnd, 1) for n in range(2, TT)}

            def after_chunk(n):
                if n < ET:
                    mha_weights_low(n)
                else:
                    if n == 2:
                        mean_squares()
                    later[n]()
                if n >= TT - 2:
                    rounded(0, n - TT + 2)
            stage_p1(0, {n: lambda n=n: after_chunk(n) for n in range(TT)})
            dve.wait_ge(rmd, 1)
            copy_rms1(0)
            dve.wait_ge(xnd, TT)
            stage_m1(0, splits(0))
            batch(0, True, True)
            with dve.Fori(1, last) as b:
                batch(b, False, True)
            batch(last, False, False)

            def top_two(tiles):
                dve.wait_ge(lgk, tiles.stop)
                for t in tiles:
                    nc.vector.max(mx[:, t, :], lg[:, t, :]).then_inc(top, 1)
                    dve.wait_ge(top, 2 * t + 1)
                    nc.vector.max_index(ix[:, t, :], mx[:, t, :], lg[:, t, :]).then_inc(top, 1)

            def gates():
                dve.wait_ge(top, 2 * TT)
                nc.vector.tensor_tensor(gate[:, 0, :], mx[:, :, 1], mx[:, :, 0], ALU.subtract).then_inc(gch, 1)
                copy(ixf[:, :, :], ix[:, :, 0:2])
                dve.wait_ge(gch, 1)
                dve.wait_ge(gex, 1)
                nc.vector.tensor_scalar(gate[:, 0, :], gate[:, 1, :], 1.0, None, ALU.add).then_inc(gch, 1)
                dve.wait_ge(gch, 2)
                nc.vector.reciprocal(gate[:, 2, :], gate[:, 0, :]).then_inc(gch, 1)
                dve.wait_ge(gch, 3)
                nc.vector.tensor_tensor(gate[:, 3, :], gate[:, 1, :], gate[:, 2, :], ALU.mult).then_inc(gch, 1)
                dve.wait_ge(gch, 4)
                dve.wait_ge(iotd, 16)
                for j in range(2):
                    nc.vector.tensor_tensor(pick[:, j, :, :], iot[:, :, :],
                                            ixf[:, :, j:j + 1].broadcast_to([P, TT, NE]), ALU.is_equal).then_inc(gch, 1)
                    dve.wait_ge(gch, 5 + 2 * j)
                    nc.vector.tensor_tensor(pick[:, j, :, :], pick[:, j, :, :],
                                            gate[:, 2 + j, :].unsqueeze(2).broadcast_to([P, TT, NE]),
                                            ALU.mult).then_inc(gch, 1)
                    dve.wait_ge(gch, 6 + 2 * j)
                nc.vector.tensor_tensor(cw[:, :, :].rearrange("p n t -> p t n"), pick[:, 0, :, :], pick[:, 1, :, :],
                                        ALU.add).then_inc(cwd, 1)
                dve.wait_ge(cwd, 1)

            def product(n, it):
                dve.wait_ge(ud, n + 1)
                dve.wait_ge(sgd, n + 1)
                nc.vector.tensor_tensor(hf[:, it % 2, :], ps[2 + it % 2][:, :], sg[:, it % 2, :],
                                        ALU.mult).then_inc(hfd, 1)
                dve.wait_ge(hfd, n + 1)
                copy(hh[:, it % 2, :], hf[:, it % 2, :]).then_inc(hhd, 1)
                dve.wait_ge(hhd, n + 1)
                minus(hl[:, it % 2, :], hf[:, it % 2, :], hh[:, it % 2, :]).then_inc(hld, 1)

            def add_y(e, c):
                dve.wait_ge(dd, 16 * e + 4 * c + 4)
                for t in range(TC // P):
                    a = xn[:, bass.ds(4 * c + t, 1), :].rearrange("p o e -> p (o e)")
                    w_ = cw[:, bass.ds(e, 1), bass.ds(4 * c + t, 1)].rearrange("p a b -> p (a b)")
                    i = nc.vector.scalar_tensor_tensor(out=a, in0=ps[4 + t // 2][:, (t % 2) * E:(t % 2 + 1) * E],
                                                       scalar=w_, in1=a, op0=ALU.mult, op1=ALU.add)
                i.then_inc(yd, 1)

            def expert(e, s, first, final):
                def chunk(c, n, between):
                    for it in range(1, IT):
                        product(n + it, it)
                        between(it - 1)
                    if not (final and c == NC - 1):
                        product(n + IT, 0)
                    add_y(e, c)
                    between(IT - 1)
                if not final:
                    c0 = 1 if first else 0
                    chunk(c0, 16 * e + 4 * c0, lambda k: split_piece(e + 1, 1 - s, k))
                    with dve.Fori(c0 + 1, NC) as c:
                        chunk(c, 16 * e + 4 * c, lambda k: None)
                else:
                    for c in range(NC):
                        chunk(c, 16 * e + 4 * c, lambda k: (c > 0 and k == 2) and result(c - 1, 4 * c - 4, 4 * c))

            def result(n, t0, t1):
                t = slice(t0, t1)
                wait(dve, xrd, 32)
                wait(dve, gld, n + 1)
                nc.vector.tensor_tensor(s_tok[:, t, :], s_tok[:, t, :], gl[:, t0 % 4:t0 % 4 + t1 - t0, :],
                                        ALU.mult).then_inc(mud, 1)
                wait(dve, mud, n + 1)
                nc.vector.tensor_tensor(xr[:, t, :], xr[:, t, :], s_tok[:, t, :], ALU.add).then_inc(fin, 1)

            normalise, kept = close2(last)
            for k in range(PIECES):
                piece_low(0, 0, k)
            normalise()
            top_two(range(EARLY))
            product(0, 0)
            kept()
            stats_x2(last)
            mean_squares2(1)
            product(1, 1)
            for t in range(EARLY, TT):
                scale_tokens(t)
            product(2, 2)
            for t in range(EARLY, TT):
                keep_columns(t)
            product(3, 3)
            for t in range(EARLY, TT):
                keep_logits(t)
            top_two(range(EARLY, TT))
            gates()
            product(4, 0)
            add_y(0, 0)
            expert(0, 0, True, False)
            expert(1, 1, False, False)
            with dve.Fori(1, NE // 2 - 1) as i:
                for s in range(2):
                    expert(2 * i + s, s, False, False)
            expert(NE - 2, 0, False, False)
            expert(NE - 1, 1, False, True)

            result(NC - 1, TT - 4, TT - 2)
            result(NC, TT - 2, TT)


def laid_out(f):
    a = {k: np.asarray(v) for k, v in f.items()}
    dt = np.float32

    def per_head(w, rows):
        return w.reshape(H, rows, w.shape[1])

    w_uqr = np.concatenate([per_head(a["L0_attn_w_qr"], RD), per_head(a["L0_attn_w_uq"], D)], 1).reshape(H * HW, CQ).T
    w_ukv = np.concatenate([a["L0_attn_w_uk"], a["L0_attn_w_uv"]], 0).T
    w_cols = np.concatenate([a["L0_attn_w_kr"], a["L0_ffn_Wq"], a["L0_ffn_Wk"], a["L0_ffn_Wv"]], 0).T

    def lhs(w):
        return w.T.reshape(ET, P, FF).transpose(1, 0, 2).reshape(P, ET * FF)

    experts = np.stack([np.concatenate([
        lhs(a["L0_ffn_Wg"][e]), lhs(a["L0_ffn_Wu"][e]),
        a["L0_ffn_Wd"][e].T.reshape(IT, P, E).transpose(1, 0, 2).reshape(P, IT * E)], 1) for e in range(NE)])

    pos = np.arange(S, dtype=dt)
    inv = (1.0 / 10000.0 ** (np.arange(0, RD, 2, dtype=dt) / RD)).astype(dt)
    ang = (pos[:, None] * inv[None, :]).astype(dt)
    c, s = np.cos(ang), np.sin(ang)
    cosines = np.concatenate([c, c, np.ones((S, D), dt)], 1).reshape(2, P, HW).transpose(1, 0, 2)
    sines = np.concatenate([-s, s], 1).reshape(2, P, RD).transpose(1, 0, 2)
    i = np.arange(P)
    mask = np.where(i[None, :] > i[:, None], BIG, 0.0)
    consts = dict(cosines=cosines, sines=sines, ident=np.eye(P), mask=mask, mask_t=mask.T, seen_t=np.where(i[:, None] > i[None, :], 0.0, BOUND),
                  experts_iota=np.broadcast_to(np.arange(NE), (P, TT, NE)))
    r = dict(
        x=a["L0_attn_x"].reshape(T, E), w_cols=w_cols, w_dq=a["L0_attn_w_dq"], w_uqr=w_uqr,
        w_dkv=a["L0_attn_w_dkv"], w_ukv=w_ukv, w_out=a["L0_attn_w_out"].T, w_o=a["L0_ffn_Wo"].T,
        w_ln1=a["L0_ffn_w_ln1"].reshape(ET, P).T, w_ln2=a["L0_ffn_w_ln2"].reshape(ET, P).T,
        w_r=a["L0_ffn_Wr"].T, w_experts=experts, **{k: v.astype(dt) for k, v in consts.items()})
    return {k: np.ascontiguousarray(v) for k, v in r.items()}


def kernel(**inputs):
    import concourse.bacc as bacc
    from concourse.bass_utils import run_bass_kernel_spmd

    nc = bacc.Bacc("TRN2", target_bir_lowering=False, num_devices=1)
    arrays = laid_out(inputs)
    args = {k: nc.dram_tensor(f"in_{k}", v.shape, mybir.dt.from_np(v.dtype), kind="ExternalInput").ap()
            for k, v in arrays.items()}
    out = nc.dram_tensor("out_0", (T, E), F32, kind="ExternalOutput").ap()
    build(nc, out=out, **args)
    r = run_bass_kernel_spmd(nc, [{f"in_{k}": v for k, v in arrays.items()}], core_ids=[0])
    return r.results[0]["out_0"].reshape(B, S, E)
```
